# Optimizing a Trainium2 kernel written in Bass

```python
import numpy as np
import jax
import jax.numpy as jnp

def _softmax(x, axis=-1):
    return jax.nn.softmax(x, axis=axis)

def _gelu(x):
    return jax.nn.gelu(x, approximate=True)

def _silu(x):
    return jax.nn.silu(x)

def _sigmoid(x):
    return jax.nn.sigmoid(x)

def _layernorm(x, axis=-1, eps=1e-05):
    m = jnp.mean(x, axis=axis, keepdims=True)
    v = jnp.var(x, axis=axis, keepdims=True)
    return (x - m) / jnp.sqrt(v + eps)

def _scatter_add(tgt, idx, src, axis=0):
    return tgt.at[idx].add(src)

def _segment_sum(src, seg, n):
    return jax.ops.segment_sum(src, seg, n)
kernel_name = 'mk_adaln_ffn_d1_seqx_r8_2f0212'

def setup_inputs(seed: int=0):
    np.random.seed(seed)
    _w = jnp.asarray

    def _rec_inputs():
        import jax
        import jax.numpy as jnp
        _rk = jax.random.key(seed)
        x = -0.0003929 + 0.9999 * jax.random.normal(jax.random.fold_in(_rk, 1), (128, 32, 512), jnp.float32)
        _lenS = 32 - jax.random.randint(jax.random.fold_in(_rk, 7), (128,), 0, max(1, 32 // 4) + 1, jnp.int32)
        _lenS2 = 32 - jax.random.randint(jax.random.fold_in(_rk, 8), (128,), 0, max(1, 32 // 4) + 1, jnp.int32)
        itok_B_78_3631 = jax.random.randint(jax.random.fold_in(_rk, 11), (128,), 78, 454, jnp.int32)
        return (x, itok_B_78_3631)
    x, itok_B_78_3631 = _rec_inputs()

    def _L0_cond_setup():
        import math
        import jax, jax.numpy as jnp
        import numpy as np
        B, H, N, L = (16, 32, 64, 512)
        DT_MIN, DT_MAX = (0.001, 0.1)

        def _get_kernel(log_dt, C, log_A_real, A_imag, length):
            dt = jnp.exp(log_dt)
            Cc = C[..., 0] + 1j * C[..., 1]
            A = -jnp.exp(log_A_real) + 1j * A_imag
            dtA = A * dt[:, None]
            Ct = Cc * (jnp.exp(dtA) - 1.0) / A
            P = dtA[:, :, None] * jnp.arange(length, dtype=jnp.float32)
            K = 2.0 * jnp.einsum('hn,hnl->hl', Ct, jnp.exp(P)).real
            return K
        key = jax.random.key(seed)
        ks = jax.random.split(key, 5)
        u = jax.random.normal(ks[0], (B, H, L), dtype=jnp.float32)
        log_dt = jax.random.uniform(ks[1], (H,), dtype=jnp.float32) * (math.log(DT_MAX) - math.log(DT_MIN)) + math.log(DT_MIN)
        C = jax.random.normal(ks[2], (H, N, 2), dtype=jnp.float32)
        log_A_real = jnp.log(0.5 * jnp.ones((H, N), dtype=jnp.float32))
        A_imag = math.pi * jnp.broadcast_to(jnp.arange(N, dtype=jnp.float32), (H, N))
        D = jax.random.normal(ks[3], (H,), dtype=jnp.float32)
        length = jax.random.randint(ks[4], (B,), 1, L + 1, dtype=jnp.int32)
        return {'u': u, 'log_dt': log_dt, 'C': C, 'log_A_real': log_A_real, 'A_imag': A_imag, 'D': D, 'length': length}
    _L0_cond_all = _L0_cond_setup()
    _L0_cond_in = {k: v for k, v in _L0_cond_all.items() if k in ('log_dt', 'C', 'log_A_real', 'A_imag', 'D')}
    del _L0_cond_all

    def _L0_ffn_setup():
        import jax, jax.numpy as jnp
        import numpy as np
        _FP8_MAX = 448.0

        def _quantize_fp8(w):
            scale = jnp.maximum(jnp.max(jnp.abs(w)).astype(jnp.float32) / _FP8_MAX, 1e-12)
            w_q = (w / scale).astype(jnp.float8_e4m3fn).astype(jnp.float32)
            return (w_q, scale)

        def _fake_quant_fp8_linear(x, w_q, in_scale, w_scale):
            x_q = jnp.clip(x / in_scale, -_FP8_MAX, _FP8_MAX)
            x_dq = x_q.astype(jnp.float8_e4m3fn).astype(jnp.float32) * in_scale
            w_dq = w_q * w_scale
            return jnp.einsum('bsh,ih->bsi', x_dq, w_dq)
        key = jax.random.key(seed)
        k_x, k_g, k_u, k_d = jax.random.split(key, 4)
        B, S, H, I = (4, 256, 512, 1376)
        x = jax.random.normal(k_x, (B, S, H), dtype=jnp.float32)
        gate = jax.random.normal(k_g, (I, H), dtype=jnp.float32) * 0.05
        up = jax.random.normal(k_u, (I, H), dtype=jnp.float32) * 0.05
        down = jax.random.normal(k_d, (H, I), dtype=jnp.float32) * 0.05
        gate_w, gate_w_scale = _quantize_fp8(gate)
        up_w, up_w_scale = _quantize_fp8(up)
        down_w, down_w_scale = _quantize_fp8(down)
        one = jnp.float32(1.0)
        return {'x': x, 'gate_w': gate_w, 'up_w': up_w, 'down_w': down_w, 'gate_w_scale': gate_w_scale, 'up_w_scale': up_w_scale, 'down_w_scale': down_w_scale, 'gate_in_scale': one, 'up_in_scale': one, 'down_in_scale': one}
    _L0_ffn_all = _L0_ffn_setup()
    _L0_ffn_in = {k: v for k, v in _L0_ffn_all.items() if k in ('gate_w', 'up_w', 'down_w', 'gate_w_scale', 'up_w_scale', 'down_w_scale', 'gate_in_scale', 'up_in_scale', 'down_in_scale')}
    del _L0_ffn_all
    return {'x': x, 'itok_B_78_3631': itok_B_78_3631, 'L0_cond_log_dt': _L0_cond_in['log_dt'], 'L0_cond_C': _L0_cond_in['C'], 'L0_cond_log_A_real': _L0_cond_in['log_A_real'], 'L0_cond_A_imag': _L0_cond_in['A_imag'], 'L0_cond_D': _L0_cond_in['D'], 'L0_ffn_gate_w': _L0_ffn_in['gate_w'], 'L0_ffn_up_w': _L0_ffn_in['up_w'], 'L0_ffn_down_w': _L0_ffn_in['down_w'], 'L0_ffn_gate_w_scale': _L0_ffn_in['gate_w_scale'], 'L0_ffn_up_w_scale': _L0_ffn_in['up_w_scale'], 'L0_ffn_down_w_scale': _L0_ffn_in['down_w_scale'], 'L0_ffn_gate_in_scale': _L0_ffn_in['gate_in_scale'], 'L0_ffn_up_in_scale': _L0_ffn_in['up_in_scale'], 'L0_ffn_down_in_scale': _L0_ffn_in['down_in_scale']}

def reference(x, itok_B_78_3631, L0_cond_log_dt, L0_cond_C, L0_cond_log_A_real, L0_cond_A_imag, L0_cond_D, L0_ffn_gate_w, L0_ffn_up_w, L0_ffn_down_w, L0_ffn_gate_w_scale, L0_ffn_up_w_scale, L0_ffn_down_w_scale, L0_ffn_gate_in_scale, L0_ffn_up_in_scale, L0_ffn_down_in_scale):
    import jax
    import jax.numpy as jnp

    def _L0_cond_ref(u, log_dt, C, log_A_real, A_imag, D, length):
        import math
        import jax, jax.numpy as jnp
        import numpy as np
        B, H, N, L = (16, 32, 64, 512)
        DT_MIN, DT_MAX = (0.001, 0.1)

        def _get_kernel(log_dt, C, log_A_real, A_imag, length):
            dt = jnp.exp(log_dt)
            Cc = C[..., 0] + 1j * C[..., 1]
            A = -jnp.exp(log_A_real) + 1j * A_imag
            dtA = A * dt[:, None]
            Ct = Cc * (jnp.exp(dtA) - 1.0) / A
            P = dtA[:, :, None] * jnp.arange(length, dtype=jnp.float32)
            K = 2.0 * jnp.einsum('hn,hnl->hl', Ct, jnp.exp(P)).real
            return K
        Bq, Hq, Lq = u.shape
        K = _get_kernel(log_dt, C, log_A_real, A_imag, Lq)
        n = 2 * Lq
        kf = jnp.fft.rfft(K, n=n)
        uf = jnp.fft.rfft(u, n=n)
        y = jnp.fft.irfft(uf * kf[None], n=n)[..., :Lq]
        y = y + u * D[:, None]
        mask = (jnp.arange(Lq)[None, :] < length[:, None]).astype(u.dtype)
        return y * mask[:, None, :]

    def _L0_ffn_ref(x, gate_w, up_w, down_w, gate_w_scale, up_w_scale, down_w_scale, gate_in_scale, up_in_scale, down_in_scale):
        import jax, jax.numpy as jnp
        import numpy as np
        _FP8_MAX = 448.0

        def _quantize_fp8(w):
            scale = jnp.maximum(jnp.max(jnp.abs(w)).astype(jnp.float32) / _FP8_MAX, 1e-12)
            w_q = (w / scale).astype(jnp.float8_e4m3fn).astype(jnp.float32)
            return (w_q, scale)

        def _fake_quant_fp8_linear(x, w_q, in_scale, w_scale):
            x_q = jnp.clip(x / in_scale, -_FP8_MAX, _FP8_MAX)
            x_dq = x_q.astype(jnp.float8_e4m3fn).astype(jnp.float32) * in_scale
            w_dq = w_q * w_scale
            return jnp.einsum('bsh,ih->bsi', x_dq, w_dq)
        gate_out = _fake_quant_fp8_linear(x, gate_w, gate_in_scale, gate_w_scale)
        up_out = _fake_quant_fp8_linear(x, up_w, up_in_scale, up_w_scale)
        hidden = jax.nn.silu(gate_out) * up_out
        return _fake_quant_fp8_linear(hidden, down_w, down_in_scale, down_w_scale)
    x = x + _L0_ffn_ref(_L0_cond_ref(x, L0_cond_log_dt, L0_cond_C, L0_cond_log_A_real, L0_cond_A_imag, L0_cond_D, itok_B_78_3631), L0_ffn_gate_w, L0_ffn_up_w, L0_ffn_down_w, L0_ffn_gate_w_scale, L0_ffn_up_w_scale, L0_ffn_down_w_scale, L0_ffn_gate_in_scale, L0_ffn_up_in_scale, L0_ffn_down_in_scale)
    return x

_drawn_inputs = setup_inputs


def setup_inputs(seed=0):
    import zlib

    import numpy as np

    out = dict(_drawn_inputs(seed))
    spreads = {'L0_cond_log_A_real': (-0.6931471824645996, 0.2)}
    factors = {}
    for name, (base, spread) in spreads.items():
        noise = np.random.default_rng([zlib.crc32(name.encode()), seed]).standard_normal(out[name].shape)
        drawn = base * np.exp(spread * noise) if base else spread * noise
        out[name] = jnp.asarray(drawn.astype(out[name].dtype))
    for name, factor in factors.items():
        out[name] = (out[name] * factor).astype(out[name].dtype)
    return out
```

```python
from contextlib import ExitStack
import math

import numpy as np

import concourse.bass as bass
from concourse import mybir

F32 = mybir.dt.float32
BF16 = mybir.dt.bfloat16
I32 = mybir.dt.int32
ALU = mybir.AluOpType
ACT = mybir.ActivationFunctionType

P = 128
B, C, L = 128, 32, 512
N = 64
I = 1376
HB = 4
NBLK = C // HB
TOK = HB * B
LB = L // P
CH = -(-I // P)
TAIL = I - (CH - 1) * P
KA, KB = 16, 32
M = KB + 2 * KA
PADK = P - 1
ROW = 640
FP8_MAX = 448.0
READ = 1
EMPTY = 2
UP20 = 2.0 ** 20
FLOOR = 1.5 * 2.0 ** 14
MAGIC = 1.5 * 2.0 ** 23
LOG2E = 1.4426950408889634
LN2_HI = 0.693145751953125
LN2_LO = 0.6931471805599453 - LN2_HI
INV_2PI = 1.0 / (2 * math.pi)
PI2_1 = 6.28125
PI2_2 = round((2 * math.pi - PI2_1) * 2 ** 20) / 2 ** 20
PI2_3 = 2 * math.pi - PI2_1 - PI2_2
PI_IN = 3.1415925


def width(c):
    return P if c < CH - 1 else TAIL


def adaln_ffn_kernel(nc, xT, xn, length, params, consts, dskip, scales, wg_d, wu_d, wd_d, out):
    kpad = nc.dram_tensor("kpad_scratch", (C, ROW), F32, kind="Internal")
    toep_d = bass.AP(kpad, 0, [[HB * ROW, NBLK], [1, P], [ROW, HB], [1, L]])

    with ExitStack() as ctx:
        def sb(name, shape, dt=F32):
            return ctx.enter_context(nc.sbuf_tensor(name, shape, dt))

        def sem(name):
            return ctx.enter_context(nc.semaphore(name))

        def bank(name):
            return ctx.enter_context(nc.psum_tensor(name, [P, 512], F32))

        gate_ps = [bank(f"gate_ps{i}") for i in range(2)]
        up_ps = [bank(f"up_ps{i}") for i in range(2)]
        down_ps = [bank(f"down_ps{i}") for i in range(2)]
        y_ps = [bank(f"y_ps{i}") for i in range(2)]

        wg = sb("wg", [P, LB, I], BF16)
        wu = sb("wu", [P, LB, I], BF16)
        wd = sb("wd", [P, CH, L], BF16)
        prm = sb("prm", [P, 5 * C])
        cst = sb("cst", [P, 2 * M + LB])
        scl = sb("scl", [P, 6])
        dsk = sb("dsk", [1, C])
        leni = sb("leni", [P, B], I32)
        lenf = sb("lenf", [P, B])
        mask = sb("mask", [P, LB, B])
        fac = sb("fac", [P, 10])
        R_GATE, R_UP, S_GATE, S_UP, S_DOWN, R_DOWN, T_UP, R_GATE20, R_UP20 = range(9)

        sm = sb("sm", [P, 40, C])
        dec = sb("dec", [P, C, KB + KA])
        e2 = sb("e2", [P, C, KB])
        g1 = sb("g1", [P, C, KA])
        g2 = sb("g2", [P, C, KA])
        krow = sb("krow", [KA, C, KB])
        zrow = sb("zrow", [C, P])

        toep = [sb(f"toep{i}", [P, HB, L]) for i in range(2)]
        xt = [sb(f"xt{i}", [P, HB, L]) for i in range(2)]
        xres = [sb(f"xres{i}", [P, HB, L]) for i in range(2)]
        osb = [sb(f"osb{i}", [P, HB, L]) for i in range(2)]
        ym = [sb(f"ym{i}", [P, L]) for i in range(2)]
        yv = [sb(f"yv{i}", [P, 2, L]) for i in range(2)]
        yc = [sb(f"yc{i}", [P, 2, L]) for i in range(2)]
        yt = [sb(f"yt{i}", [P, 2, L]) for i in range(2)]
        yq = [sb(f"yq{i}", [P, 2, LB, TOK], BF16) for i in range(2)]
        sil = [sb(f"sil{i}", [P, TOK]) for i in range(2)]
        hv = [sb(f"hv{i}", [P, TOK]) for i in range(2)]
        hc = [sb(f"hc{i}", [P, TOK]) for i in range(2)]
        ht = [sb(f"ht{i}", [P, TOK]) for i in range(2)]
        hq = [sb(f"hq{i}", [P, CH, TOK], BF16) for i in range(2)]
        ang = osb[0][:].rearrange("p h l -> p (h l)").rearrange("p (c m) -> p c m", m=M)
        turns = osb[1][:].rearrange("p h l -> p (h l)").rearrange("p (c m) -> p c m", m=M)
        sinv = hq[1][:].rearrange("p k n -> p (k n)").bitcast(F32)[:, 0:C * M].rearrange("p (c m) -> p c m", m=M)

        params_in, consts_in, scales_in = sem("params_in"), sem("consts_in"), sem("scales_in")
        weights_in = sem("weights_in")
        conv_in = [sem(f"conv_in{i}") for i in range(2)]
        xres_in = [sem(f"xres_in{i}") for i in range(2)]
        chain = sem("chain")
        zeros_set, k_stored = sem("zeros_set"), sem("k_stored")
        small_ang_ready, small_sin_ready = sem("small_ang_ready"), sem("small_sin_ready")
        ang_ready, sin_ready = sem("ang_ready"), sem("sin_ready")
        dec_arg_ready, dec_ready = sem("dec_arg_ready"), sem("dec_ready")
        factors_ready, k_ready, kroabs_ready, kprod_ready = (
            sem("factors_ready"), sem("k_ready"), sem("kroabs_ready"), sem("kprod_ready"))
        gate_ready, up_ready, silu_done = sem("gate_ready"), sem("up_ready"), sem("silu_done")
        prod_done, clip_done, abs_ready = sem("prod_done"), sem("clip_done"), sem("abs_ready")
        t_done, hq_ready = sem("t_done"), sem("hq_ready")
        y_ready, ym_done, yscaled = sem("y_ready"), sem("ym_done"), sem("yscaled")
        ymagic_done, yt_done, yq_ready = sem("ymagic_done"), sem("yt_done"), sem("yq_ready")
        down_ready, out_done = sem("down_ready"), sem("out_done")
        stored = [sem(f"stored{i}") for i in range(2)]

        def at_least(eng, s, v):
            if not (isinstance(v, int) and v <= 0):
                eng.wait_ge(s, v)

        block = ctx.enter_context(nc.Block())

        @block.sync
        def _(sp):
            sp.dma_start(prm[:], params).then_inc(params_in, 16)
            sp.dma_start(cst[:], consts).then_inc(consts_in, 16)
            sp.dma_start(scl[:], scales.partition_broadcast(P)).then_inc(scales_in, 16)
            sp.dma_start(leni[:], length.partition_broadcast(P)).then_inc(scales_in, 16)
            sp.dma_start(dsk[:], dskip).then_inc(scales_in, 16)
            sp.wait_ge(zeros_set, 1)
            for i in range(2):
                rows = slice(i * C // 2, (i + 1) * C // 2)
                sp.dma_start(kpad.ap()[rows, 0:PADK], zrow[rows, 0:PADK]).then_inc(stored[i], 16)

            def load_x_t(g, par):
                sp.dma_start(xt[par][:], xT[g]).then_inc(conv_in[par], 16)

            def load_toep(g, par):
                sp.dma_start(toep[par][:], toep_d[g]).then_inc(conv_in[par], 16)

            def load_res(g, par):
                sp.dma_start(xres[par][:], xn[:, bass.ts(g, HB), :]).then_inc(xres_in[par], 16)

            def store(g, par):
                sp.dma_start(out[:, bass.ts(g, HB), :], osb[par][:]).then_inc(stored[par], 16)

            load_x_t(0, 0)
            load_x_t(1, 1)
            sp.wait_ge(kroabs_ready, 2)
            sp.dma_start(bass.AP(kpad, PADK, [[KB, KA], [ROW, C], [1, KB]]), krow[:]).then_inc(k_stored, 16)
            sp.wait_ge(stored[0], 16)
            sp.wait_ge(stored[1], 16)
            sp.wait_ge(k_stored, 16)
            load_toep(0, 0)
            load_toep(1, 1)
            load_res(0, 0)
            load_res(1, 1)

            def next_conv(g, par):
                at_least(sp, y_ready, HB * (g - 1))
                load_x_t(g, par)
                load_toep(g, par)

            def turn(g, par, conv):
                at_least(sp, out_done, EMPTY + HB * (g - 1))
                store(g - 2, par)
                load_res(g, par)
                if conv:
                    next_conv(g + 2, par)

            next_conv(2, 0)
            next_conv(3, 1)
            with sp.Fori(0, (NBLK - 4) // 2) as j:
                turn(2 * j + 2, 0, True)
                turn(2 * j + 3, 1, True)
            turn(NBLK - 2, 0, False)
            turn(NBLK - 1, 1, False)
            sp.wait_ge(out_done, EMPTY + HB * (NBLK - 1))
            store(NBLK - 2, 0)
            for t in range(HB):
                sp.wait_ge(out_done, EMPTY + HB * (NBLK - 1) + t + 1)
                sp.dma_start(out[:, HB * (NBLK - 1) + t, :], osb[1][:, t, :]).then_inc(stored[1], 16)
            sp.wait_ge(stored[0], 16 * (NBLK // 2 + 1))
            sp.wait_ge(stored[1], 16 * (NBLK // 2 + HB))

        @block.gpsimd
        def _(pool):
            nc.gpsimd.memset(zrow[:], 0.0).then_inc(zeros_set, 1)
            pool.dma_start(wg[:], wg_d).then_inc(weights_in, 16)
            pool.dma_start(wu[:], wu_d).then_inc(weights_in, 16)
            pool.dma_start(wd[:, 0:CH - 1, :],
                           wd_d[0:(CH - 1) * P, :].rearrange("(k p) n -> p k n", p=P)).then_inc(weights_in, 16)
            pool.dma_start(wd[0:TAIL, CH - 1, :], wd_d[(CH - 1) * P:I, :]).then_inc(weights_in, 16)

            def round_y(g, par, h):
                m = HB * g + h
                q = h % 2
                at_least(pool, ymagic_done, m + 1)
                nc.gpsimd.tensor_tensor(yt[q][:], yv[q][:], yc[q][:], ALU.add).then_inc(yt_done, 1)
                at_least(pool, yt_done, m + 1)
                at_least(pool, up_ready, CH * (g - 1))
                nc.gpsimd.tensor_tensor(
                    yq[par][:, :, :, h * B:(h + 1) * B],
                    yt[q][:].rearrange("p v (k b) -> p v k b", k=LB),
                    yc[q][:].rearrange("p v (k b) -> p v k b", k=LB), ALU.subtract).then_inc(yq_ready, 1)

            for g in (0, 1):
                for h in range(HB):
                    round_y(g, g, h)
            with pool.Fori(0, (NBLK - 2) // 2) as j:
                for h in range(HB):
                    round_y(2 * j + 2, 0, h)
                for h in range(HB):
                    round_y(2 * j + 3, 1, h)

        @block.scalar
        def _(act):
            act.wait_ge(small_ang_ready, 1)
            nc.scalar.activation(sm[:, 12:14, :], sm[:, 10:12, :], ACT.Sin).then_inc(small_sin_ready, 1)
            act.wait_ge(dec_arg_ready, 2)
            nc.scalar.activation(dec[:], dec[:], ACT.Exp).then_inc(dec_ready, 1)
            act.wait_ge(ang_ready, 1)
            nc.scalar.activation(sinv, ang, ACT.Sin).then_inc(sin_ready, 1)
            for i in range(2):
                act.wait_ge(k_ready, 1)
                nc.scalar.copy(krow[:, 16 * i:16 * i + 16, :],
                               gate_ps[i][0:KA, :].rearrange("p (h b) -> p h b", b=KB)).then_inc(kprod_ready, 1)

            def scale_y(g, h):
                m = HB * g + h
                q = h % 2
                at_least(act, ym_done, m + 1)
                at_least(act, yq_ready, m - 1)
                nc.scalar.activation(yv[q][:, 0, :], ym[q][:], ACT.Copy, scale=fac[:, R_GATE:R_GATE + 1])
                nc.scalar.activation(yv[q][:, 1, :], ym[q][:], ACT.Copy, scale=fac[:, R_UP:R_UP + 1])
                nc.scalar.activation(yc[q][:, 0, :], ym[q][:], ACT.Abs, scale=fac[:, R_GATE20:R_GATE20 + 1])
                nc.scalar.activation(yc[q][:, 1, :], ym[q][:], ACT.Abs,
                                     scale=fac[:, R_UP20:R_UP20 + 1]).then_inc(yscaled, 1)

            def abs_prod(n, par, c):
                b = (par + c) % 2
                w = width(c)
                at_least(act, clip_done, n + 1)
                at_least(act, hq_ready, n - 1)
                nc.scalar.activation(hc[b][0:w, :], hv[b][0:w, :], ACT.Abs, scale=UP20).then_inc(abs_ready, 1)

            def slots(g, par, first, ahead):
                for c in range(CH):
                    n = CH * g + c
                    b = (par + c) % 2
                    w = width(c)
                    if c:
                        abs_prod(n - 1, par, c - 1)
                    elif not first:
                        abs_prod(n - 1, 1 - par, CH - 1)
                    at_least(act, gate_ready, n + 1)
                    at_least(act, prod_done, n - 1)
                    nc.scalar.activation(sil[b][0:w, :], gate_ps[b][0:w, :], ACT.Silu,
                                         scale=fac[0:w, S_GATE:S_GATE + 1]).then_inc(silu_done, 1)
                    if ahead and c in SCALE_PLAN:
                        scale_y(g + 1, SCALE_PLAN[c][1])

            act.wait_ge(factors_ready, 1)
            for h in range(HB):
                scale_y(0, h)
            slots(0, 0, True, 2)
            with act.Fori(0, (NBLK - 2) // 2) as j:
                slots(2 * j + 1, 1, False, 2)
                slots(2 * j + 2, 0, False, 2)
            slots(NBLK - 1, 1, False, 0)
            abs_prod(CH * NBLK - 1, 1, CH - 1)

        @block.tensor
        def _(pe):
            pe.wait_ge(factors_ready, 3)
            for h in range(C):
                last = nc.tensor.matmul(gate_ps[h // 16][0:KA, (h % 16) * KB:(h % 16 + 1) * KB],
                                        g1[:, h, :], e2[:, h, :], start=True, stop=True)
                if h == 0:
                    last.then_inc(down_ready, READ)
            last.then_inc(k_ready, 1)

            def conv(g, par, half, h, distances):
                m = HB * g + h
                if distances[0] == 0:
                    if h == 0:
                        at_least(pe, conv_in[par], 32 * (half + 1))
                    at_least(pe, ym_done, m - 1)
                for d in distances:
                    last = nc.tensor.matmul(y_ps[h % 2][:, d * P:L], toep[par][:, h, d * P:(d + 1) * P],
                                            xt[par][:, h, 0:L - d * P], start=(d == 0), stop=(d == 2))
                if d == 2:
                    last.then_inc(y_ready, 1)

            def down_part(g, par, c):
                for s in range(HB * c, HB * (c + 1)):
                    t, k = divmod(s, CH)
                    w = width(k)
                    if t == 0:
                        at_least(pe, hq_ready, CH * g + k + 1)
                    if k == 0:
                        at_least(pe, out_done, EMPTY + HB * g + t - 1)
                    mm = nc.tensor.matmul(down_ps[t % 2][:], hq[par][0:w, k, t * P:(t + 1) * P],
                                          wd[0:w, k, :], start=(k == 0), stop=(k == CH - 1))
                    if k == CH - 1:
                        mm.then_inc(down_ready, 1)

            def slots(g, par, half, down, ahead):
                for c in range(CH):
                    n = CH * g + c
                    b = (par + c) % 2
                    w = width(c)
                    if c == 0:
                        at_least(pe, yq_ready, HB * (g + 1))
                    at_least(pe, silu_done, n - 1)
                    for k in range(LB):
                        mm = nc.tensor.matmul(gate_ps[b][0:w, :], wg[:, k, c * P:c * P + w],
                                              yq[par][:, 0, k, :], start=(k == 0), stop=(k == LB - 1))
                    mm.then_inc(gate_ready, 1)
                    at_least(pe, prod_done, n - 1)
                    for k in range(LB):
                        mm = nc.tensor.matmul(up_ps[b][0:w, :], wu[:, k, c * P:c * P + w],
                                              yq[par][:, 1, k, :], start=(k == 0), stop=(k == LB - 1))
                    mm.then_inc(up_ready, 1)
                    for step, h, distances in CONV_PLAN.get(c, ()):
                        if step <= ahead:
                            conv(g + step, (par + step) % 2, half + (1 if step == 2 else par), h, distances)
                    if down:
                        down_part(g - 1, 1 - par, c)

            for h in range(HB):
                conv(0, 0, 0, h, [0, 1, 3, 2])
            conv(1, 1, 0, 0, [0, 1, 3, 2])
            conv(1, 1, 0, 1, [0])
            pe.wait_ge(weights_in, 64)
            slots(0, 0, 0, False, 2)
            with pe.Fori(0, (NBLK - 4) // 2) as j:
                slots(2 * j + 1, 1, j, True, 2)
                slots(2 * j + 2, 0, j + 1, True, 2)
            slots(NBLK - 3, 1, (NBLK - 3) // 2, True, 2)
            slots(NBLK - 2, 0, (NBLK - 2) // 2, True, 1)
            slots(NBLK - 1, 1, None, True, 0)
            for c in range(CH):
                down_part(NBLK - 1, 1, c)

        @block.vector
        def _(dve):
            v = nc.vector
            done = [0]

            def link(ins):
                done[0] += 1
                ins.then_inc(chain, 1)
                dve.wait_ge(chain, done[0])

            def s(i, n=1):
                return sm[:, i:i + n, :]

            def minus_one(i_q, i_two_k, i_out, n):
                link(v.tensor_tensor(s(i_out, n), s(i_q, n), s(i_two_k, n), ALU.mult))
                link(v.scalar_tensor_tensor(s(i_out, n), s(i_two_k, n), -1.0, s(i_out, n), ALU.add, ALU.add))

            def exp_parts(x, kf, r, q, two_k, n):
                link(v.tensor_scalar(x, x, -87.0, 88.0, ALU.max, ALU.min))
                link(v.tensor_scalar(kf, x, LOG2E, MAGIC, ALU.mult, ALU.add))
                link(v.tensor_scalar(kf, kf, MAGIC, None, ALU.subtract))
                link(v.scalar_tensor_tensor(r, kf, -LN2_HI, x, ALU.mult, ALU.add))
                link(v.scalar_tensor_tensor(r, kf, -LN2_LO, r, ALU.mult, ALU.add))
                link(v.tensor_scalar(q, r, 1.0 / math.factorial(8), None, ALU.mult))
                for d in range(7, 0, -1):
                    link(v.scalar_tensor_tensor(q, q, 1.0 / math.factorial(d), r, ALU.add, ALU.mult))
                link(v.tensor_scalar(two_k.bitcast(I32), kf, 127.0, 2.0 ** 23, ALU.add, ALU.mult))

            v.memset(fac[:], 0.0).then_inc(out_done, EMPTY)
            dve.wait_ge(params_in, 16)
            pr = prm[:].rearrange("p (f h) -> p f h", f=5)
            exp_parts(pr[:, 0:2, :], s(0, 2), s(2, 2), s(4, 2), s(6, 2), 2)
            link(v.scalar_tensor_tensor(s(8, 2), s(4, 2), 1.0, s(6, 2), ALU.add, ALU.mult))
            link(v.scalar_tensor_tensor(s(14), s(9), -1.0, s(8), ALU.mult, ALU.mult))
            link(v.tensor_tensor(s(15), pr[:, 2:3, :], s(8), ALU.mult))
            link(v.tensor_scalar(s(16), s(15), 0.5, None, ALU.mult))

            def reduce_angle(out_ap, a, t):
                link(v.scalar_tensor_tensor(out_ap, t, -PI2_1, a, ALU.mult, ALU.add))
                link(v.scalar_tensor_tensor(out_ap, t, -PI2_2, out_ap, ALU.mult, ALU.add))
                link(v.scalar_tensor_tensor(out_ap, t, -PI2_3, out_ap, ALU.mult, ALU.add))

            link(v.tensor_scalar(s(17, 2), s(15, 2), INV_2PI, MAGIC, ALU.mult, ALU.add))
            link(v.tensor_scalar(s(17, 2), s(17, 2), MAGIC, None, ALU.subtract))
            reduce_angle(s(10, 2), s(15, 2), s(17, 2))
            v.tensor_scalar(s(10, 2), s(10, 2), PI_IN, -PI_IN, ALU.min, ALU.max).then_inc(small_ang_ready, 1)
            dve.wait_ge(consts_in, 16)

            def by_h(ap, m):
                return ap.rearrange("p o h -> p h o").broadcast_to([P, C, m])

            def by_m(lo, m):
                return cst[:, lo:lo + m].rearrange("p (o m) -> p o m", o=1).broadcast_to([P, C, m])

            v.tensor_tensor(dec[:, :, 0:KB], by_h(s(14), KB), by_m(0, KB), ALU.mult).then_inc(dec_arg_ready, 1)
            v.tensor_tensor(dec[:, :, KB:], by_h(s(14), KA), by_m(KB, KA), ALU.mult).then_inc(dec_arg_ready, 1)
            link(v.tensor_tensor(ang, by_h(s(15), M), by_m(0, M), ALU.mult))
            link(v.scalar_tensor_tensor(turns, ang, INV_2PI, by_m(M, M), ALU.mult, ALU.add))
            link(v.tensor_scalar(turns, turns, MAGIC, MAGIC, ALU.add, ALU.subtract))
            reduce_angle(ang, ang, turns)
            link(v.scalar_tensor_tensor(ang, by_m(M, M), 2 * math.pi, ang, ALU.mult, ALU.add))
            v.tensor_scalar(ang, ang, PI_IN, -PI_IN, ALU.min, ALU.max).then_inc(ang_ready, 1)

            exp_parts(s(14), s(20), s(21), s(22), s(23), 1)
            minus_one(22, 23, 24, 1)
            link(v.tensor_scalar(s(25), s(24), 1.0, None, ALU.add))
            dve.wait_ge(small_sin_ready, 1)
            link(v.scalar_tensor_tensor(s(26), s(13), -2.0, s(13), ALU.mult, ALU.mult))
            link(v.tensor_tensor(s(26), s(26), s(25), ALU.mult))
            link(v.tensor_tensor(s(26), s(26), s(24), ALU.add))
            link(v.tensor_tensor(s(27), s(12), s(25), ALU.mult))
            cr, ci = pr[:, 3:4, :], pr[:, 4:5, :]
            v.tensor_tensor(s(28), cr, s(26), ALU.mult)
            v.tensor_tensor(s(29), ci, s(27), ALU.mult)
            v.tensor_tensor(s(30), cr, s(27), ALU.mult)
            link(v.tensor_tensor(s(31), ci, s(26), ALU.mult))
            link(v.tensor_tensor(s(28), s(28), s(29), ALU.subtract))
            link(v.tensor_tensor(s(30), s(30), s(31), ALU.add))
            ai = pr[:, 2:3, :]
            v.tensor_tensor(s(32), s(9), s(9), ALU.mult)
            link(v.tensor_tensor(s(33), ai, ai, ALU.mult))
            link(v.tensor_tensor(s(32), s(32), s(33), ALU.add))
            link(v.reciprocal(s(32), s(32)))
            v.tensor_tensor(s(34), s(30), ai, ALU.mult)
            v.tensor_tensor(s(35), s(28), s(9), ALU.mult)
            v.tensor_tensor(s(36), s(30), s(9), ALU.mult)
            link(v.tensor_tensor(s(37), s(28), ai, ALU.mult))
            link(v.tensor_tensor(s(34), s(34), s(35), ALU.subtract))
            link(v.tensor_tensor(s(36), s(36), s(37), ALU.add))
            link(v.tensor_tensor(s(34), s(34), s(32), ALU.mult))
            link(v.tensor_tensor(s(36), s(36), s(32), ALU.mult))
            v.tensor_scalar(sm[0:N, 38, :], sm[0:N, 34, :], 2.0, None, ALU.mult)
            v.tensor_scalar(sm[0:N, 39, :], sm[0:N, 36, :], 2.0, None, ALU.mult)
            v.tensor_scalar(sm[N:P, 38, :], sm[N:P, 36, :], 2.0, None, ALU.mult)
            link(v.tensor_scalar(sm[N:P, 39, :], sm[N:P, 34, :], -2.0, None, ALU.mult))
            dve.wait_ge(dec_ready, 1)
            dve.wait_ge(sin_ready, 1)
            v.tensor_tensor(e2[:], sinv[:, :, 0:KB], dec[:, :, 0:KB], ALU.mult).then_inc(factors_ready, 1)
            v.tensor_tensor(g1[:], sinv[:, :, KB:KB + KA], by_h(s(38), KA), ALU.mult)
            link(v.tensor_tensor(g2[:], sinv[:, :, KB + KA:M], by_h(s(39), KA), ALU.mult))
            link(v.tensor_tensor(g1[:], g1[:], g2[:], ALU.add))
            v.tensor_tensor(g1[:], g1[:], dec[:, :, KB:], ALU.mult).then_inc(factors_ready, 1)

            def f(i):
                return fac[:, i:i + 1]

            def sc(i):
                return scl[:, i:i + 1]

            dve.wait_ge(scales_in, 48)
            v.reciprocal(f(R_GATE), sc(0))
            v.reciprocal(f(R_UP), sc(1))
            v.reciprocal(f(R_DOWN), sc(2))
            v.tensor_tensor(f(S_GATE), sc(0), sc(3), ALU.mult)
            v.tensor_tensor(f(T_UP), sc(1), sc(4), ALU.mult)
            link(v.tensor_tensor(f(S_DOWN), sc(2), sc(5), ALU.mult))
            v.tensor_tensor(f(S_UP), f(T_UP), f(R_DOWN), ALU.mult)
            v.tensor_scalar(f(R_GATE20), f(R_GATE), UP20, None, ALU.mult)
            link(v.tensor_scalar(f(R_UP20), f(R_UP), UP20, None, ALU.mult))
            link(v.tensor_copy(lenf[:], leni[:]))
            for k in range(LB):
                last = v.tensor_scalar(mask[:, k, :], lenf[:], cst[:, 2 * M + k:2 * M + k + 1], None, ALU.is_gt)
            link(last)
            v.tensor_copy(lenf[:, 0:1], lenf[:, 0:1]).then_inc(factors_ready, 1)

            dve.wait_ge(kprod_ready, 2)
            v.tensor_tensor(krow[0:1, :, 0], krow[0:1, :, 0], dsk[:], ALU.add).then_inc(kroabs_ready, 2)

            def mask_y(g, h):
                m = HB * g + h
                q = h % 2
                at_least(dve, y_ready, m + 1)
                at_least(dve, yscaled, m - 1)
                v.tensor_tensor(ym[q][:], y_ps[q][:], mask[:].rearrange("p k b -> p (k b)"),
                                ALU.mult).then_inc(ym_done, 1)

            def magic_y(g, h):
                m = HB * g + h
                q = h % 2
                at_least(dve, yscaled, m + 1)
                v.tensor_scalar(yv[q][:], yv[q][:], FP8_MAX, -FP8_MAX, ALU.min, ALU.max)
                v.tensor_scalar(yc[q][:], yc[q][:], FLOOR, FP8_MAX * UP20, ALU.max, ALU.min).then_inc(ymagic_done, 1)

            def rounded_sum(n, par, c):
                b, w = (par + c) % 2, width(c)
                at_least(dve, abs_ready, n + 1)
                v.scalar_tensor_tensor(ht[b][0:w, :], hc[b][0:w, :], FLOOR, hv[b][0:w, :],
                                       ALU.max, ALU.add).then_inc(t_done, 1)

            def rounded(n, par, g, c):
                b, w = (par + c) % 2, width(c)
                at_least(dve, t_done, n + 1)
                if c == 0:
                    at_least(dve, down_ready, READ + HB * (g - 1))
                v.scalar_tensor_tensor(hq[par][0:w, c, :], hc[b][0:w, :], FLOOR, ht[b][0:w, :],
                                       ALU.max, ALU.subtract, reverse1=True).then_inc(hq_ready, 1)

            def residual(g, par, half, t):
                if t == 0:
                    at_least(dve, xres_in[par], 16 * (half + 1))
                    at_least(dve, stored[par], 16 * (half + 1))
                at_least(dve, down_ready, READ + HB * g + t + 1)
                v.scalar_tensor_tensor(osb[par][:, t, :], down_ps[t % 2][:], f(S_DOWN), xres[par][:, t, :],
                                       ALU.mult, ALU.add).then_inc(out_done, 1)

            def slots(g, par, prev_half, first, ahead):
                for c in range(CH):
                    n = CH * g + c
                    b, w = (par + c) % 2, width(c)
                    before = (n - 1, par, g, c - 1) if c else (n - 1, 1 - par, g - 1, CH - 1)
                    lag = c > 0 or not first
                    if lag:
                        rounded_sum(before[0], before[1], before[3])
                    at_least(dve, silu_done, n + 1)
                    at_least(dve, up_ready, n + 1)
                    v.scalar_tensor_tensor(hv[b][0:w, :], up_ps[b][0:w, :], fac[0:w, S_UP:S_UP + 1], sil[b][0:w, :],
                                           ALU.mult, ALU.mult).then_inc(prod_done, 1)
                    if lag:
                        rounded(*before)
                    at_least(dve, prod_done, n + 1)
                    v.tensor_scalar(hv[b][0:w, :], hv[b][0:w, :], FP8_MAX, -FP8_MAX,
                                    ALU.min, ALU.max).then_inc(clip_done, 1)
                    if c in MASK_PLAN and MASK_PLAN[c][0] <= ahead:
                        mask_y(g + MASK_PLAN[c][0], MASK_PLAN[c][1])
                    if ahead and c in MAGIC_PLAN:
                        magic_y(g + 1, MAGIC_PLAN[c][1])
                    if not first and c in OUT_SLOTS:
                        residual(g - 1, 1 - par, prev_half, OUT_SLOTS.index(c))

            for h in range(HB):
                mask_y(0, h)
                if h:
                    magic_y(0, h - 1)
            magic_y(0, HB - 1)
            mask_y(1, 0)
            slots(0, 0, None, True, 2)
            with dve.Fori(0, (NBLK - 4) // 2) as j:
                slots(2 * j + 1, 1, j, False, 2)
                slots(2 * j + 2, 0, j, False, 2)
            slots(NBLK - 3, 1, NBLK // 2 - 2, False, 2)
            slots(NBLK - 2, 0, NBLK // 2 - 2, False, 1)
            slots(NBLK - 1, 1, NBLK // 2 - 1, False, 0)
            last_n = CH * NBLK - 1
            rounded_sum(last_n, 1, CH - 1)
            rounded(last_n, 1, NBLK - 1, CH - 1)
            for t in range(HB):
                residual(NBLK - 1, 1, NBLK // 2 - 1, t)


CONV_PLAN = {
    8: [(2, 0, [0])], 9: [(2, 0, [1, 3])], 10: [(2, 0, [2]), (2, 1, [0])],
    0: [(1, 1, [1, 3])], 1: [(1, 1, [2])],
    2: [(1, 2, [0])], 3: [(1, 2, [1, 3])], 4: [(1, 2, [2]), (1, 3, [0])],
    5: [(1, 3, [1, 3])], 6: [(1, 3, [2])],
}
MASK_PLAN = {10: (2, 0), 1: (1, 1), 4: (1, 2), 6: (1, 3)}
SCALE_PLAN = {0: (1, 0), 2: (1, 1), 5: (1, 2), 7: (1, 3)}
MAGIC_PLAN = {1: (1, 0), 3: (1, 1), 6: (1, 2), 8: (1, 3)}
OUT_SLOTS = [3, 6, 9, 10]


def trig_constants():
    t = np.zeros((P, 2 * M + LB), np.float32)
    t[:, 0:KB] = np.arange(KB)
    t[:, KB:KB + KA] = KB * np.arange(KA)
    t[:, KB + KA:M] = KB * np.arange(KA)
    t[0:N, M:M + KB] = 0.25
    t[:, M + KB:M + KB + KA] = 0.25
    t[:, 2 * M:] = np.arange(P)[:, None] + P * np.arange(LB)[None, :]
    return t


def kernel(**inputs):
    import concourse.bacc as bacc
    from concourse.bass_utils import run_bass_kernel_spmd

    a = {k: np.asarray(v) for k, v in inputs.items()}
    x = a["x"]
    xt = x.transpose(1, 2, 0).reshape(NBLK, HB, LB, P, B)[:, :, :, ::-1, :]
    xt = xt.transpose(0, 3, 1, 2, 4).reshape(NBLK, P, HB, L)

    def both(z):
        return np.concatenate([z.T, z.T], axis=0)

    params = np.concatenate([
        np.broadcast_to(a["L0_cond_log_dt"][None, :], (P, C)), both(a["L0_cond_log_A_real"]),
        both(a["L0_cond_A_imag"]), both(a["L0_cond_C"][..., 0]), both(a["L0_cond_C"][..., 1])], axis=1)
    scales = np.stack([a[f"L0_ffn_{n}"].reshape(()) for n in
                       ("gate_in_scale", "up_in_scale", "down_in_scale", "gate_w_scale", "up_w_scale", "down_w_scale")])

    def by_k(w):
        return w.T.reshape(LB, P, I).transpose(1, 0, 2)

    arrays = {
        "in_xT": xt, "in_x": x, "in_length": a["itok_B_78_3631"], "in_params": params, "in_consts": trig_constants(),
        "in_D": a["L0_cond_D"].reshape(1, C), "in_scales": scales,
        "in_gate": by_k(a["L0_ffn_gate_w"]), "in_up": by_k(a["L0_ffn_up_w"]), "in_down": a["L0_ffn_down_w"].T,
    }
    nc = bacc.Bacc("TRN2", target_bir_lowering=False, num_devices=1)
    arrays = {k: np.ascontiguousarray(z) for k, z in arrays.items()}
    args = [nc.dram_tensor(k, z.shape, mybir.dt.from_np(z.dtype), kind="ExternalInput").ap() for k, z in arrays.items()]
    args.append(nc.dram_tensor("out", (B, C, L), F32, kind="ExternalOutput").ap())
    adaln_ffn_kernel(nc, *args)
    r = run_bass_kernel_spmd(nc, [arrays], core_ids=[0])
    return r.results[0]["out"]
```

```python
from contextlib import ExitStack
import math

import numpy as np

import concourse.bass as bass
from concourse import mybir

F32 = mybir.dt.float32
F32R = mybir.dt.float32r
BF16 = mybir.dt.bfloat16
I32 = mybir.dt.int32
ALU = mybir.AluOpType
ACT = mybir.ActivationFunctionType

P = 128
B, C, L = 128, 32, 512
N = 64
I = 1376
HB = 4
NBLK = C // HB
TOK = HB * B
LB = L // P
CH = -(-I // P)
TAIL = I - (CH - 1) * P
KA, KB = 16, 32
M = KB + KA
PADK = P - 1
ROW = 640
FP8_MAX = 448.0
K_GROUPS = [range(0, 4), range(4, 16), range(16, 32)]
WARM = 14
READ = 1
EMPTY = 2
UP20 = 2.0 ** 20
FLOOR = 1.5 * 2.0 ** 14
MAGIC = 1.5 * 2.0 ** 23
LOG2E = 1.4426950408889634
LN2_HI = 0.693145751953125
LN2_LO = 0.6931471805599453 - LN2_HI
INV_2PI = 1.0 / (2 * math.pi)
PI2_1 = 6.28125
PI2_2 = 2 * math.pi - PI2_1
PI_IN = 3.1415925


def width(c):
    return P if c < CH - 1 else TAIL


def adaln_ffn_kernel(nc, xT, xn, length, params, consts, dskip, scales, wg_d, wu_d, wd_d, out):
    kpad = nc.dram_tensor("kpad_scratch", (2, C, ROW), F32, kind="Internal")
    toep_d = [bass.AP(kpad, i * C * ROW, [[HB * ROW, NBLK], [1, P], [ROW, HB], [1, L]]) for i in range(2)]

    with ExitStack() as ctx:
        def sb(name, shape, dt=F32):
            return ctx.enter_context(nc.sbuf_tensor(name, shape, dt))

        def sem(name):
            return ctx.enter_context(nc.semaphore(name))

        def bank(name):
            return ctx.enter_context(nc.psum_tensor(name, [P, 512], F32))

        gate_ps = [bank(f"gate_ps{i}") for i in range(2)]
        up_ps = [bank(f"up_ps{i}") for i in range(2)]
        down_ps = [bank(f"down_ps{i}") for i in range(2)]
        y_ps = [bank(f"y_ps{i}") for i in range(2)]

        wg = sb("wg", [P, LB, I], BF16)
        wu = sb("wu", [P, LB, I], BF16)
        wd = sb("wd", [P, CH, L], BF16)
        prm = sb("prm", [P, 5 * C])
        cst = sb("cst", [P, M + 5 + LB])
        scl = sb("scl", [P, 6])
        dsk = sb("dsk", [1, C])
        leni = sb("leni", [P, B], I32)
        lenf = sb("lenf", [P, B])
        mask = sb("mask", [P, LB, B])
        fac = sb("fac", [P, 10])
        R_GATE, R_UP, S_GATE, S_UP, S_DOWN, R_DOWN, T_UP, R_GATE20, R_UP20 = range(9)

        sm = sb("sm", [P, 40, C])
        zrow = sb("zrow", [C, P])

        toep = [sb(f"toep{i}", [P, 2, HB, L]) for i in range(2)]
        xhi = [sb(f"xhi{i}", [P, L], F32R) for i in range(2)]
        xlo = [sb(f"xlo{i}", [P, L], F32R) for i in range(2)]
        xt = [sb(f"xt{i}", [P, HB, L]) for i in range(2)]
        xres = [sb(f"xres{i}", [P, HB, L]) for i in range(2)]
        osb = [sb(f"osb{i}", [P, HB, L]) for i in range(2)]
        ym = [sb(f"ym{i}", [P, L]) for i in range(2)]
        yv = [sb(f"yv{i}", [P, 2, L]) for i in range(2)]
        yc = [sb(f"yc{i}", [P, 2, L]) for i in range(2)]
        yt = sb("yt", [P, 2, L])
        yq = [sb(f"yq{i}", [P, 2, LB, TOK], BF16) for i in range(2)]
        sil = [sb(f"sil{i}", [P, TOK]) for i in range(2)]
        hv = [sb(f"hv{i}", [P, TOK]) for i in range(2)]
        hc = [sb(f"hc{i}", [P, TOK]) for i in range(2)]
        ht = sb("ht", [P, TOK])
        hq = [sb(f"hq{i}", [P, CH, TOK], BF16) for i in range(2)]

        def inside(tile, lo, n):
            flat = tile[:].rearrange("p a b -> p (a b)")
            flat = flat if flat.dtype == F32 else flat.bitcast(F32)
            return flat[:, C * lo:C * (lo + n)].rearrange("p (c m) -> p c m", m=n)

        ang, g1 = inside(osb[0], 0, M), inside(osb[0], M, KA)
        turns, g2 = inside(osb[1], 0, M), inside(osb[1], M, KA)
        dec, e2 = inside(hq[0], 0, M), inside(hq[0], M, KB)
        esin, gcos, gsin = inside(hq[1], 0, KB), inside(hq[1], KB, KA), inside(hq[1], KB + KA, KA)
        krow = [inside(xres[1], i * KB, KB)[0:KA] for i in range(2)]

        params_in, consts_in, scales_in = sem("params_in"), sem("consts_in"), sem("scales_in")
        weights_in = sem("weights_in")
        xt_in = [sem(f"xt_in{i}") for i in range(2)]
        conv_in = [sem(f"conv_in{i}") for i in range(2)]
        xres_in = [sem(f"xres_in{i}") for i in range(2)]
        chain = sem("chain")
        zeros_set, k_stored = sem("zeros_set"), [sem(f"k_stored{i}") for i in range(len(K_GROUPS))]
        toep_first = [sem(f"toep_first{h}") for h in range(HB)]
        parts_ready, decay_ready, gabs_ready = sem("parts_ready"), sem("decay_ready"), sem("gabs_ready")
        small_ang_ready, small_sin_ready = sem("small_ang_ready"), sem("small_sin_ready")
        ang_ready, sin_ready = sem("ang_ready"), sem("sin_ready")
        dec_arg_ready, dec_ready, norm_ready = sem("dec_arg_ready"), sem("dec_ready"), sem("norm_ready")
        pool_chain = sem("pool_chain")
        e2_ready, g_ready, scales_ready = sem("e2_ready"), sem("g_ready"), sem("scales_ready")
        k_ready, skip_added, khi_ready, klo_ready = (
            sem("k_ready"), sem("skip_added"), sem("khi_ready"), sem("klo_ready"))
        gate_ready, up_ready, silu_done = sem("gate_ready"), sem("up_ready"), sem("silu_done")
        prod_done, clip_done, abs_ready = sem("prod_done"), sem("clip_done"), sem("abs_ready")
        t_done, hq_ready = sem("t_done"), sem("hq_ready")
        y_ready, ym_done, yscaled = sem("y_ready"), sem("ym_done"), sem("yscaled")
        ymagic_done, yt_done, yq_ready = sem("ymagic_done"), sem("yt_done"), sem("yq_ready")
        yq_first = sem("yq_first")
        xhi_ready, xlo_ready, xlo_first = sem("xhi_ready"), sem("xlo_ready"), sem("xlo_first")
        down_ready, out_done = sem("down_ready"), sem("out_done")
        stored = [sem(f"stored{i}") for i in range(2)]

        def at_least(eng, s, v):
            if not (isinstance(v, int) and v <= 0):
                eng.wait_ge(s, v)

        def k_in_bank(i):
            hs = K_GROUPS[i]
            bank = (down_ps[0], down_ps[1], y_ps[1])[i]
            return (bank[0:KA, 0:len(hs) * KB].rearrange("p (h b) -> p h b", b=KB), slice(hs[0], hs[-1] + 1))

        block = ctx.enter_context(nc.Block())

        @block.sync
        def _(sp):
            sp.dma_start(prm[:], params).then_inc(params_in, 16)
            sp.dma_start(cst[:], consts).then_inc(consts_in, 16)
            sp.dma_start(scl[:], scales.partition_broadcast(P)).then_inc(scales_in, 16)
            sp.dma_start(leni[:], length.partition_broadcast(P)).then_inc(scales_in, 16)
            sp.dma_start(dsk[:], dskip).then_inc(scales_in, 16)
            sp.wait_ge(zeros_set, 1)
            for i in range(2):
                sp.dma_start(bass.AP(kpad, i * C * ROW, [[ROW, C], [1, PADK]]), zrow[:, 0:PADK]).then_inc(stored[i], 16)

            def load_x_t(g, par):
                sp.dma_start(xt[par][:], xT[g]).then_inc(xt_in[par], 16)

            def load_toep(g, par):
                for i in range(2):
                    sp.dma_start(toep[par][:, i], toep_d[i][g]).then_inc(conv_in[par], 16)

            def load_res(g, par):
                sp.dma_start(xres[par][:], xn[:, bass.ts(g, HB), :]).then_inc(xres_in[par], 16)

            def store(g, par):
                sp.dma_start(out[:, bass.ts(g, HB), :], osb[par][:]).then_inc(stored[par], 16)

            load_x_t(0, 0)
            load_x_t(1, 1)
            sp.wait_ge(stored[0], 16)
            sp.wait_ge(stored[1], 16)

            def store_k(b):
                lo, n = K_GROUPS[b][0], len(K_GROUPS[b])
                for i in range(2):
                    sp.wait_ge((khi_ready, klo_ready)[i], b + 1)
                    sp.dma_start(bass.AP(kpad, (i * C + lo) * ROW + PADK, [[KB, KA], [ROW, n], [1, KB]]),
                                 krow[i][:, lo:lo + n, :]).then_inc(k_stored[b], 16)

            store_k(0)
            sp.wait_ge(k_stored[0], 32)
            for h in range(HB):
                for i in range(2):
                    sp.dma_start(toep[0][:, i, h], toep_d[i][0, :, h]).then_inc(toep_first[h], 16)
            store_k(1)
            store_k(2)
            load_res(0, 0)
            sp.wait_ge(k_stored[1], 32)
            load_toep(1, 1)
            sp.wait_ge(k_stored[2], 32)
            load_res(1, 1)

            def next_conv(g, par):
                at_least(sp, y_ready, HB * (g - 1))
                load_x_t(g, par)
                load_toep(g, par)

            def turn(g, par, conv):
                at_least(sp, out_done, EMPTY + HB * (g - 1))
                store(g - 2, par)
                load_res(g, par)
                if conv:
                    next_conv(g + 2, par)

            next_conv(2, 0)
            next_conv(3, 1)
            with sp.Fori(0, (NBLK - 4) // 2) as j:
                turn(2 * j + 2, 0, True)
                turn(2 * j + 3, 1, True)
            turn(NBLK - 2, 0, False)
            turn(NBLK - 1, 1, False)
            sp.wait_ge(out_done, EMPTY + HB * (NBLK - 1))
            store(NBLK - 2, 0)
            for t in range(HB):
                sp.wait_ge(out_done, EMPTY + HB * (NBLK - 1) + t + 1)
                sp.dma_start(out[:, HB * (NBLK - 1) + t, :], osb[1][:, t, :]).then_inc(stored[1], 16)
            sp.wait_ge(stored[0], 16 * (NBLK // 2 + 1))
            sp.wait_ge(stored[1], 16 * (NBLK // 2 + HB))

        @block.gpsimd
        def _(pool):
            nc.gpsimd.memset(zrow[:], 0.0).then_inc(zeros_set, 1)
            pool.dma_start(wg[:], wg_d).then_inc(weights_in, 16)
            pool.dma_start(wu[:], wu_d).then_inc(weights_in, 16)
            pool.dma_start(wd[:, 0:CH - 1, :],
                           wd_d[0:(CH - 1) * P, :].rearrange("(k p) n -> p k n", p=P)).then_inc(weights_in, 16)
            pool.dma_start(wd[0:TAIL, CH - 1, :], wd_d[(CH - 1) * P:I, :]).then_inc(weights_in, 16)

            count = [0]

            def link(ins):
                count[0] += 1
                ins.then_inc(pool_chain, 1)
                pool.wait_ge(pool_chain, count[0])

            gp = nc.gpsimd
            pool.wait_ge(decay_ready, 1)
            def s(i):
                return sm[:, i, :]

            link(gp.tensor_scalar(s(19), s(14), -87.0, None, ALU.max))
            link(gp.tensor_scalar(s(20), s(19), LOG2E, MAGIC, ALU.mult, ALU.add))
            link(gp.tensor_scalar(s(20), s(20), MAGIC, None, ALU.subtract))
            for ln2 in (LN2_HI, LN2_LO):
                link(gp.tensor_scalar(s(21), s(20), ln2, None, ALU.mult))
                link(gp.tensor_tensor(s(19), s(19), s(21), ALU.subtract))
            link(gp.tensor_scalar(s(22), s(19), 1.0 / math.factorial(7), None, ALU.mult))
            for d in range(6, 0, -1):
                link(gp.tensor_scalar(s(22), s(22), 1.0 / math.factorial(d), None, ALU.add))
                link(gp.tensor_tensor(s(22), s(22), s(19), ALU.mult))
            link(gp.tensor_scalar(s(23).bitcast(I32), s(20), 127.0, 2.0 ** 23, ALU.add, ALU.mult))
            link(gp.tensor_tensor(s(22), s(22), s(23), ALU.mult))
            link(gp.tensor_scalar(s(23), s(23), -1.0, None, ALU.add))
            link(gp.tensor_tensor(s(24), s(22), s(23), ALU.add))
            gp.tensor_scalar(s(25), s(24), 1.0, None, ALU.add)
            cr, ci, ai = (prm[:, i * C:(i + 1) * C] for i in (3, 4, 2))
            gp.tensor_tensor(s(34), ci, ai, ALU.mult)
            gp.tensor_tensor(s(35), cr, s(9), ALU.mult)
            gp.tensor_tensor(s(36), cr, ai, ALU.mult)
            link(gp.tensor_tensor(s(37), ci, s(9), ALU.mult))
            gp.tensor_tensor(s(34), s(34), s(35), ALU.subtract)
            link(gp.tensor_tensor(s(36), s(36), s(37), ALU.add))
            pool.wait_ge(norm_ready, 1)
            gp.tensor_tensor(s(34), s(34), s(32), ALU.mult)
            gp.tensor_tensor(s(36), s(36), s(32), ALU.mult).then_inc(parts_ready, 1)
            pool.wait_ge(dec_ready, 1)
            pool.wait_ge(sin_ready, 1)
            gp.tensor_tensor(e2, esin, dec[:, :, 0:KB], ALU.mult).then_inc(e2_ready, 1)

            def split_x(g, par, h):
                m = HB * g + h
                at_least(pool, xhi_ready, m + 1)
                nc.gpsimd.tensor_tensor(xlo[h % 2][:], xt[par][:, h, :], xhi[h % 2][:].bitcast(F32),
                                        ALU.subtract).then_inc(xlo_ready, 1)

            def round_y(g, par, h, versions=2):
                m = HB * g + h
                q = h % 2
                n = versions
                at_least(pool, ymagic_done, m + 1)
                at_least(pool, yq_ready, m)
                nc.gpsimd.tensor_tensor(yt[:, 0:n], yv[q][:, 0:n], yc[q][:, 0:n], ALU.add).then_inc(yt_done, 1)
                at_least(pool, yt_done, m + 1)
                at_least(pool, up_ready, CH * (g - 1))
                nc.gpsimd.tensor_tensor(
                    yq[par][:, 0:n, :, h * B:(h + 1) * B],
                    yt[:, 0:n].rearrange("p v (k b) -> p v k b", k=LB),
                    yc[q][:, 0:n].rearrange("p v (k b) -> p v k b", k=LB), ALU.subtract).then_inc(yq_ready, 1)

            def turn(g, par, ahead):
                split_x(g, par, 3)
                round_y(g, par, 0)
                round_y(g, par, 1)
                if ahead:
                    split_x(g + 1, 1 - par, 0)
                round_y(g, par, 2)
                if ahead:
                    split_x(g + 1, 1 - par, 1)
                round_y(g, par, 3)
                if ahead:
                    split_x(g + 1, 1 - par, 2)

            split_x(0, 0, 0)
            split_x(0, 0, 1)
            split_x(0, 0, 2)
            split_x(0, 0, 3)
            for h in range(HB):
                round_y(0, 0, h, 1)
            split_x(1, 1, 2)
            turn(1, 1, True)
            with pool.Fori(0, (NBLK - 4) // 2) as j:
                turn(2 * j + 2, 0, True)
                turn(2 * j + 3, 1, True)
            turn(NBLK - 2, 0, True)
            turn(NBLK - 1, 1, False)

        @block.scalar
        def _(act):
            act.wait_ge(dec_arg_ready, 1)
            nc.scalar.activation(dec, dec, ACT.Exp).then_inc(dec_ready, 1)
            act.wait_ge(small_ang_ready, 1)
            nc.scalar.activation(sm[:, 12:14, :], sm[:, 10:12, :], ACT.Sin).then_inc(small_sin_ready, 1)
            act.wait_ge(ang_ready, 2)
            nc.scalar.activation(gcos, ang[:, :, KB:], ACT.Abs).then_inc(gabs_ready, 1)
            nc.scalar.activation(esin, ang[:, :, 0:KB], ACT.Sin, bias=cst[:, M:M + 1]).then_inc(sin_ready, 1)
            nc.scalar.activation(gsin, ang[:, :, KB:], ACT.Sin).then_inc(sin_ready, 1)
            act.wait_ge(gabs_ready, 1)
            nc.scalar.activation(gcos, gcos, ACT.Sin, bias=cst[:, M + 4:M + 5], scale=-1.0).then_inc(sin_ready, 1)

            def split_x(g, par, half, h):
                m = HB * g + h
                if h == 0:
                    at_least(act, xt_in[par], 16 * (half + 1))
                at_least(act, y_ready, m - 1)
                nc.scalar.copy(xhi[h % 2][:], xt[par][:, h, :]).then_inc(xhi_ready, 1)

            split_x(0, 0, 0, 0)
            split_x(0, 0, 0, 1)
            for i in range(len(K_GROUPS)):
                act.wait_ge(skip_added, i + 1)
                k_all, hs = k_in_bank(i)
                nc.scalar.copy(krow[0][:, hs, :].bitcast(F32R), k_all).then_inc(khi_ready, 1)

            def scale_y(g, h):
                m = HB * g + h
                q = h % 2
                at_least(act, ym_done, m + 1)
                at_least(act, yt_done, m - 1)
                if isinstance(m, int) and 2 <= m < 2 + HB:
                    act.wait_ge(yq_first, m - 1)
                nc.scalar.activation(yv[q][:, 0, :], ym[q][:], ACT.Copy, scale=fac[:, R_GATE:R_GATE + 1])
                nc.scalar.activation(yv[q][:, 1, :], ym[q][:], ACT.Copy, scale=fac[:, R_UP:R_UP + 1])
                at_least(act, yq_ready, m - 1)
                nc.scalar.activation(yc[q][:, 0, :], ym[q][:], ACT.Abs, scale=fac[:, R_GATE20:R_GATE20 + 1])
                nc.scalar.activation(yc[q][:, 1, :], ym[q][:], ACT.Abs,
                                     scale=fac[:, R_UP20:R_UP20 + 1]).then_inc(yscaled, 1)

            def abs_prod(n, par, c):
                b = (par + c) % 2
                w = width(c)
                at_least(act, clip_done, n + 1)
                at_least(act, hq_ready, n - 1)
                nc.scalar.activation(hc[b][0:w, :], hv[b][0:w, :], ACT.Abs, scale=UP20).then_inc(abs_ready, 1)

            def slots(g, par, half, first, ahead):
                for c in range(CH):
                    n = CH * g + c
                    b = (par + c) % 2
                    w = width(c)
                    at_least(act, gate_ready, n + 1)
                    at_least(act, prod_done, n - 1)
                    nc.scalar.activation(sil[b][0:w, :], gate_ps[b][0:w, :], ACT.Silu,
                                         scale=fac[0:w, S_GATE:S_GATE + 1]).then_inc(silu_done, 1)
                    if c:
                        abs_prod(n - 1, par, c - 1)
                    elif not first:
                        abs_prod(n - 1, 1 - par, CH - 1)
                    if c in SPLIT_PLAN and SPLIT_PLAN[c][0] <= ahead:
                        step, h = SPLIT_PLAN[c]
                        split_x(g + step, (par + step) % 2, half + (1 if step == 2 else par), h)
                    if ahead and c in SCALE_PLAN:
                        scale_y(g + 1, SCALE_PLAN[c][1])

            act.wait_ge(scales_ready, 1)
            split_x(0, 0, 0, 2)
            scale_y(0, 0)
            split_x(0, 0, 0, 3)
            scale_y(0, 1)
            split_x(1, 1, 0, 0)
            scale_y(0, 2)
            split_x(1, 1, 0, 1)
            scale_y(0, 3)
            split_x(1, 1, 0, 2)
            slots(0, 0, 0, True, 2)
            with act.Fori(0, (NBLK - 4) // 2) as j:
                slots(2 * j + 1, 1, j, False, 2)
                slots(2 * j + 2, 0, j + 1, False, 2)
            slots(NBLK - 3, 1, (NBLK - 3) // 2, False, 2)
            slots(NBLK - 2, 0, (NBLK - 2) // 2, False, 1)
            slots(NBLK - 1, 1, None, False, 0)
            abs_prod(CH * NBLK - 1, 1, CH - 1)

        @block.tensor
        def _(pe):
            pe.wait_ge(e2_ready, 1)
            pe.wait_ge(g_ready, 1)
            for i, hs in enumerate(K_GROUPS):
                for h in hs:
                    last = nc.tensor.matmul(k_in_bank(i)[0][:, h - hs[0]], g1[:, h], e2[:, h], start=True, stop=True)
                last.then_inc(k_ready, 1)
            pe.wait_ge(weights_in, 64)
            for n in range(WARM):
                last = nc.tensor.matmul(up_ps[n % 2][:], wg[:, 0, 0:P], wg[:, 0, 0:512], start=True, stop=True)
            last.then_inc(down_ready, READ)

            def conv(g, par, half, h, distances):
                m = HB * g + h
                if distances[0] == 0:
                    if isinstance(m, int) and m < HB:
                        pe.wait_ge(toep_first[h], 32)
                    elif h == 0:
                        at_least(pe, conv_in[par], 32 * (half + par))
                    at_least(pe, ym_done, m - 1)
                    if isinstance(m, int) and HB <= m < HB + 2:
                        pe.wait_ge(xlo_first, m - HB + 1)
                    else:
                        at_least(pe, xlo_ready, m + 1 if isinstance(m, int) and m < HB else m - 1)
                for d in distances:
                    for part, x in ((0, xhi), (0, xlo), (1, xhi)):
                        last = nc.tensor.matmul(y_ps[h % 2][:, d * P:L],
                                                toep[par][:, part, h, d * P:(d + 1) * P].bitcast(F32R),
                                                x[h % 2][:, 0:L - d * P], start=(d == 0 and part == 0 and x is xhi),
                                                stop=(d == 2 and part == 1))
                if d == 2:
                    last.then_inc(y_ready, 1)

            def down_part(g, par, c):
                for s in range(HB * c, HB * (c + 1)):
                    t, k = divmod(s, CH)
                    w = width(k)
                    if t == 0:
                        at_least(pe, hq_ready, CH * g + k + 1)
                    if k == 0:
                        at_least(pe, out_done, EMPTY + HB * g + t - 1)
                    mm = nc.tensor.matmul(down_ps[t % 2][:], hq[par][0:w, k, t * P:(t + 1) * P],
                                          wd[0:w, k, :], start=(k == 0), stop=(k == CH - 1))
                    if k == CH - 1:
                        mm.then_inc(down_ready, 1)

            def by_channel(h):
                pe.wait_ge(yq_ready, h + 1)
                pe.wait_ge(yq_first, h + 1)
                cols = slice(h * B, (h + 1) * B)
                for c in range(2):
                    for ps, wt, version, ready in ((gate_ps, wg, 0, gate_ready), (up_ps, wu, 1, up_ready)):
                        for k in range(LB):
                            mm = nc.tensor.matmul(ps[c][:, cols], wt[:, k, c * P:(c + 1) * P],
                                                  yq[0][:, version, k, cols], start=(k == 0), stop=(k == LB - 1))
                        if h == HB - 1:
                            mm.then_inc(ready, 1)

            def slots(g, par, half, down, ahead):
                for c in range(CH):
                    n = CH * g + c
                    b = (par + c) % 2
                    w = width(c)
                    if c == 0:
                        at_least(pe, yq_ready, HB * (g + 1))
                    if not (isinstance(n, int) and n < 2):
                        at_least(pe, silu_done, n - 1)
                        for k in range(LB):
                            mm = nc.tensor.matmul(gate_ps[b][0:w, :], wg[:, k, c * P:c * P + w],
                                                  yq[par][:, 0, k, :], start=(k == 0), stop=(k == LB - 1))
                        mm.then_inc(gate_ready, 1)
                        at_least(pe, prod_done, n - 1)
                        for k in range(LB):
                            mm = nc.tensor.matmul(up_ps[b][0:w, :], wu[:, k, c * P:c * P + w],
                                                  yq[par][:, 1, k, :], start=(k == 0), stop=(k == LB - 1))
                        mm.then_inc(up_ready, 1)
                    for step, h, distances in CONV_PLAN.get(c, ()):
                        if step <= ahead:
                            conv(g + step, (par + step) % 2, half + (1 if step == 2 else par), h, distances)
                    if down:
                        down_part(g - 1, 1 - par, c)

            conv(0, 0, 0, 0, [0, 1, 3, 2])
            pe.wait_ge(khi_ready, len(K_GROUPS))
            pe.wait_ge(klo_ready, len(K_GROUPS))
            for h in range(1, HB):
                conv(0, 0, 0, h, [0, 1, 3, 2])
            by_channel(0)
            by_channel(1)
            conv(1, 1, 0, 0, [0, 1, 3, 2])
            by_channel(2)
            conv(1, 1, 0, 1, [0, 1, 3])
            by_channel(3)
            slots(0, 0, 0, False, 2)
            with pe.Fori(0, (NBLK - 4) // 2) as j:
                slots(2 * j + 1, 1, j, True, 2)
                slots(2 * j + 2, 0, j + 1, True, 2)
            slots(NBLK - 3, 1, (NBLK - 3) // 2, True, 2)
            slots(NBLK - 2, 0, (NBLK - 2) // 2, True, 1)
            slots(NBLK - 1, 1, None, True, 0)
            for c in range(CH):
                down_part(NBLK - 1, 1, c)

        @block.vector
        def _(dve):
            v = nc.vector
            done = [0]

            def link(ins):
                done[0] += 1
                ins.then_inc(chain, 1)
                dve.wait_ge(chain, done[0])

            def s(i, n=1):
                return sm[:, i:i + n, :]

            def exp_parts(x, kf, r, q, two_k):
                link(v.tensor_scalar(x, x, -87.0, 88.0, ALU.max, ALU.min))
                link(v.tensor_scalar(kf, x, LOG2E, MAGIC, ALU.mult, ALU.add))
                link(v.tensor_scalar(kf, kf, MAGIC, None, ALU.subtract))
                link(v.scalar_tensor_tensor(r, kf, -LN2_HI, x, ALU.mult, ALU.add))
                link(v.scalar_tensor_tensor(r, kf, -LN2_LO, r, ALU.mult, ALU.add))
                link(v.tensor_scalar(q, r, 1.0 / math.factorial(7), None, ALU.mult))
                for d in range(6, 0, -1):
                    link(v.scalar_tensor_tensor(q, q, 1.0 / math.factorial(d), r, ALU.add, ALU.mult))
                link(v.tensor_scalar(two_k.bitcast(I32), kf, 127.0, 2.0 ** 23, ALU.add, ALU.mult))

            v.memset(fac[:], 0.0).then_inc(out_done, EMPTY)
            dve.wait_ge(params_in, 16)
            pr = prm[:].rearrange("p (f h) -> p f h", f=5)
            exp_parts(pr[:, 0:2, :], s(0, 2), s(2, 2), s(4, 2), s(6, 2))
            link(v.scalar_tensor_tensor(s(8, 2), s(4, 2), 1.0, s(6, 2), ALU.add, ALU.mult))
            v.scalar_tensor_tensor(s(14), s(9), -1.0, s(8), ALU.mult, ALU.mult).then_inc(decay_ready, 1)
            link(v.tensor_tensor(s(15), pr[:, 2:3, :], s(8), ALU.mult))
            dve.wait_ge(consts_in, 16)

            def by_h(ap, m):
                return ap.rearrange("p o h -> p h o").broadcast_to([P, C, m])

            multipliers = cst[:, 0:M].rearrange("p (o m) -> p o m", o=1).broadcast_to([P, C, M])
            v.tensor_tensor(dec, by_h(s(14), M), multipliers, ALU.mult).then_inc(dec_arg_ready, 1)
            v.tensor_tensor(ang, by_h(s(15), M), multipliers, ALU.mult)
            ai = pr[:, 2:3, :]
            v.scalar_tensor_tensor(s(32), s(9), 0.5, s(9), ALU.mult, ALU.mult)
            v.scalar_tensor_tensor(s(33), ai, 0.5, ai, ALU.mult, ALU.mult)
            link(v.tensor_scalar(s(16), s(15), 0.5, None, ALU.mult))
            ang_b, ang_a, turns_b, turns_a = ang[:, :, 0:KB], ang[:, :, KB:], turns[:, :, 0:KB], turns[:, :, KB:]
            v.tensor_scalar(turns_b, ang_b, INV_2PI, cst[:, M + 1:M + 2], ALU.mult, ALU.add)
            v.tensor_scalar(turns_a, ang_a, INV_2PI, MAGIC, ALU.mult, ALU.add)
            v.tensor_tensor(s(32), s(32), s(33), ALU.add)
            link(v.tensor_scalar(s(17, 2), s(15, 2), INV_2PI, MAGIC, ALU.mult, ALU.add))
            v.reciprocal(s(32), s(32)).then_inc(norm_ready, 1)
            v.tensor_scalar(turns_b, turns_b, MAGIC, MAGIC, ALU.add, ALU.subtract)
            v.tensor_scalar(turns_a, turns_a, MAGIC, None, ALU.subtract)
            link(v.tensor_scalar(s(17, 2), s(17, 2), MAGIC, None, ALU.subtract))
            v.scalar_tensor_tensor(ang, turns, -PI2_1, ang, ALU.mult, ALU.add)
            link(v.scalar_tensor_tensor(s(10, 2), s(17, 2), -PI2_1, s(15, 2), ALU.mult, ALU.add))
            v.scalar_tensor_tensor(ang, turns, -PI2_2, ang, ALU.mult, ALU.add)
            link(v.scalar_tensor_tensor(s(10, 2), s(17, 2), -PI2_2, s(10, 2), ALU.mult, ALU.add))
            v.tensor_scalar(s(10, 2), s(10, 2), PI_IN, -PI_IN, ALU.min, ALU.max).then_inc(small_ang_ready, 1)
            v.tensor_scalar(ang_a, ang_a, PI_IN, -PI_IN, ALU.min, ALU.max).then_inc(ang_ready, 1)
            v.tensor_scalar(ang_b, ang_b, cst[:, M + 2:M + 3], cst[:, M + 3:M + 4], ALU.min, ALU.max).then_inc(ang_ready, 1)

            def f(i):
                return fac[:, i:i + 1]

            def sc(i):
                return scl[:, i:i + 1]

            dve.wait_ge(scales_in, 48)
            v.reciprocal(f(R_GATE), sc(0))
            v.reciprocal(f(R_UP), sc(1))
            v.reciprocal(f(R_DOWN), sc(2))
            v.tensor_tensor(f(S_GATE), sc(0), sc(3), ALU.mult)
            v.tensor_tensor(f(T_UP), sc(1), sc(4), ALU.mult)
            link(v.tensor_tensor(f(S_DOWN), sc(2), sc(5), ALU.mult))
            v.tensor_tensor(f(S_UP), f(T_UP), f(R_DOWN), ALU.mult)
            v.tensor_scalar(f(R_GATE20), f(R_GATE), UP20, None, ALU.mult)
            link(v.tensor_scalar(f(R_UP20), f(R_UP), UP20, None, ALU.mult))

            dve.wait_ge(parts_ready, 1)
            dve.wait_ge(small_sin_ready, 1)
            link(v.scalar_tensor_tensor(s(26), s(13), -2.0, s(13), ALU.mult, ALU.mult))
            v.tensor_tensor(s(27), s(12), s(25), ALU.mult)
            link(v.tensor_tensor(s(26), s(26), s(25), ALU.mult))
            link(v.tensor_tensor(s(26), s(26), s(24), ALU.add))
            v.tensor_tensor(s(29), s(36), s(27), ALU.mult)
            v.tensor_tensor(s(31), s(34), s(27), ALU.mult)
            v.tensor_tensor(s(28), s(34), s(26), ALU.mult)
            link(v.tensor_tensor(s(30), s(36), s(26), ALU.mult))
            v.tensor_tensor(sm[0:N, 38, :], sm[0:N, 28, :], sm[0:N, 29, :], ALU.add)
            v.tensor_tensor(sm[0:N, 39, :], sm[0:N, 30, :], sm[0:N, 31, :], ALU.subtract)
            v.tensor_tensor(sm[N:P, 38, :], sm[N:P, 30, :], sm[N:P, 31, :], ALU.subtract)
            link(v.scalar_tensor_tensor(sm[N:P, 39, :], sm[N:P, 28, :], -1.0, sm[N:P, 29, :], ALU.mult, ALU.subtract))
            dve.wait_ge(dec_ready, 1)
            dve.wait_ge(sin_ready, 3)
            v.tensor_tensor(g1, gcos, by_h(s(38), KA), ALU.mult)
            link(v.tensor_tensor(g2, gsin, by_h(s(39), KA), ALU.mult))
            link(v.tensor_tensor(g1, g1, g2, ALU.add))
            v.tensor_tensor(g1, g1, dec[:, :, KB:], ALU.mult).then_inc(g_ready, 1)

            link(v.tensor_copy(lenf[:], leni[:]))
            for k in range(LB):
                last = v.tensor_scalar(mask[:, k, :], lenf[:], cst[:, M + 5 + k:M + 6 + k], None, ALU.is_gt)
            link(last)
            v.tensor_copy(lenf[:, 0:1], lenf[:, 0:1]).then_inc(scales_ready, 1)

            for i in range(len(K_GROUPS)):
                dve.wait_ge(k_ready, i + 1)
                k_all, hs = k_in_bank(i)
                k0 = k_all[0:1, :, 0]
                v.tensor_tensor(k0, k0, dsk[:, hs], ALU.add).then_inc(skip_added, 1)
                dve.wait_ge(khi_ready, i + 1)
                v.tensor_tensor(krow[1][:, hs, :].bitcast(F32R), k_all, krow[0][:, hs, :],
                                ALU.subtract).then_inc(klo_ready, 1)

            def mask_y(g, h):
                m = HB * g + h
                q = h % 2
                at_least(dve, y_ready, m + 1)
                at_least(dve, yscaled, m - 1)
                v.tensor_tensor(ym[q][:], y_ps[q][:], mask[:].rearrange("p k b -> p (k b)"),
                                ALU.mult).then_inc(ym_done, 1)

            def magic_y(g, h):
                m = HB * g + h
                q = h % 2
                at_least(dve, yscaled, m + 1)
                v.tensor_scalar(yv[q][:], yv[q][:], FP8_MAX, -FP8_MAX, ALU.min, ALU.max)
                v.tensor_scalar(yc[q][:], yc[q][:], FLOOR, FP8_MAX * UP20, ALU.max, ALU.min).then_inc(ymagic_done, 1)

            def first_up(h):
                q = h % 2
                dve.wait_ge(ymagic_done, h + 1)
                link(v.tensor_tensor(ht[:], yv[q][:, 1], yc[q][:, 1], ALU.add))
                v.tensor_tensor(yq[0][:, 1, :, h * B:(h + 1) * B], ht[:].rearrange("p (k b) -> p k b", k=LB),
                                yc[q][:, 1].rearrange("p (k b) -> p k b", k=LB), ALU.subtract).then_inc(yq_first, 1)

            def rounded_sum(n, par, c):
                b, w = (par + c) % 2, width(c)
                at_least(dve, abs_ready, n + 1)
                at_least(dve, hq_ready, n)
                v.scalar_tensor_tensor(ht[0:w, :], hc[b][0:w, :], FLOOR, hv[b][0:w, :],
                                       ALU.max, ALU.add).then_inc(t_done, 1)

            def rounded(n, par, g, c):
                b, w = (par + c) % 2, width(c)
                at_least(dve, t_done, n + 1)
                if c == 0:
                    at_least(dve, down_ready, READ + HB * (g - 1))
                v.scalar_tensor_tensor(hq[par][0:w, c, :], hc[b][0:w, :], FLOOR, ht[0:w, :],
                                       ALU.max, ALU.subtract, reverse1=True).then_inc(hq_ready, 1)

            def residual(g, par, half, t):
                if t == 0:
                    at_least(dve, xres_in[par], 16 * (half + 1))
                    at_least(dve, stored[par], 16 * (half + 1))
                at_least(dve, down_ready, READ + HB * g + t + 1)
                v.scalar_tensor_tensor(osb[par][:, t, :], down_ps[t % 2][:], f(S_DOWN), xres[par][:, t, :],
                                       ALU.mult, ALU.add).then_inc(out_done, 1)

            def slots(g, par, prev_half, first, ahead):
                for c in range(CH):
                    n = CH * g + c
                    b, w = (par + c) % 2, width(c)
                    before = (n - 1, par, g, c - 1) if c else (n - 1, 1 - par, g - 1, CH - 1)
                    lag = c > 0 or not first
                    at_least(dve, silu_done, n + 1)
                    at_least(dve, up_ready, n + 1)
                    v.scalar_tensor_tensor(hv[b][0:w, :], up_ps[b][0:w, :], fac[0:w, S_UP:S_UP + 1], sil[b][0:w, :],
                                           ALU.mult, ALU.mult).then_inc(prod_done, 1)
                    if lag:
                        rounded_sum(before[0], before[1], before[3])
                    at_least(dve, prod_done, n + 1)
                    v.tensor_scalar(hv[b][0:w, :], hv[b][0:w, :], FP8_MAX, -FP8_MAX,
                                    ALU.min, ALU.max).then_inc(clip_done, 1)
                    if lag:
                        rounded(*before)
                    if c in MASK_PLAN and MASK_PLAN[c][0] <= ahead:
                        mask_y(g + MASK_PLAN[c][0], MASK_PLAN[c][1])
                    if ahead and c in MAGIC_PLAN:
                        magic_y(g + 1, MAGIC_PLAN[c][1])
                    if not first and c in OUT_SLOTS:
                        residual(g - 1, 1 - par, prev_half, OUT_SLOTS.index(c))

            mask_y(0, 0)
            for h in range(HB):
                if h < HB - 1:
                    mask_y(0, h + 1)
                magic_y(0, h)
                first_up(h)
                if h in (1, 2):
                    dve.wait_ge(xhi_ready, HB + h)
                    v.tensor_tensor(xlo[h - 1][:], xt[1][:, h - 1, :], xhi[h - 1][:].bitcast(F32),
                                    ALU.subtract).then_inc(xlo_first, 1)
            mask_y(1, 0)
            slots(0, 0, None, True, 2)
            with dve.Fori(0, (NBLK - 4) // 2) as j:
                slots(2 * j + 1, 1, j, False, 2)
                slots(2 * j + 2, 0, j, False, 2)
            slots(NBLK - 3, 1, NBLK // 2 - 2, False, 2)
            slots(NBLK - 2, 0, NBLK // 2 - 2, False, 1)
            slots(NBLK - 1, 1, NBLK // 2 - 1, False, 0)
            last_n = CH * NBLK - 1
            rounded_sum(last_n, 1, CH - 1)
            rounded(last_n, 1, NBLK - 1, CH - 1)
            for t in range(HB):
                residual(NBLK - 1, 1, NBLK // 2 - 1, t)


CONV_PLAN = {
    7: [(2, 0, [0])], 8: [(2, 0, [1, 3])], 9: [(2, 0, [2]), (2, 1, [0])], 10: [(2, 1, [1, 3])],
    0: [(1, 1, [2])], 1: [(1, 2, [0])], 2: [(1, 2, [1, 3])], 3: [(1, 2, [2]), (1, 3, [0])],
    4: [(1, 3, [1, 3])], 5: [(1, 3, [2])],
}
SPLIT_PLAN = {4: (2, 0), 6: (2, 1), 10: (2, 2), 1: (1, 3)}
MASK_PLAN = {9: (2, 0), 0: (1, 1), 3: (1, 2), 5: (1, 3)}
SCALE_PLAN = {0: (1, 0), 1: (1, 1), 4: (1, 2), 6: (1, 3)}
MAGIC_PLAN = {1: (1, 0), 2: (1, 1), 5: (1, 2), 7: (1, 3)}
OUT_SLOTS = [3, 6, 9, 10]


def trig_constants():
    t = np.zeros((P, M + 5 + LB), np.float32)
    t[:, 0:KB] = np.arange(KB)
    t[:, KB:M] = KB * np.arange(KA)
    phase = np.where(np.arange(P) < N, math.pi / 2, 0.0)
    t[:, M] = phase
    t[:, M + 1] = phase / (2 * math.pi)
    t[:, M + 2] = PI_IN - phase
    t[:, M + 3] = -PI_IN - phase
    t[:, M + 4] = math.pi / 2
    t[:, M + 5:] = np.arange(P)[:, None] + P * np.arange(LB)[None, :]
    return t


def kernel(**inputs):
    import concourse.bacc as bacc
    from concourse.bass_utils import run_bass_kernel_spmd

    a = {k: np.asarray(v) for k, v in inputs.items()}
    x = a["x"]
    xt = x.transpose(1, 2, 0).reshape(NBLK, HB, LB, P, B)[:, :, :, ::-1, :]
    xt = xt.transpose(0, 3, 1, 2, 4).reshape(NBLK, P, HB, L)

    def both(z):
        return np.concatenate([z.T, z.T], axis=0)

    params = np.concatenate([
        np.broadcast_to(a["L0_cond_log_dt"][None, :], (P, C)), both(a["L0_cond_log_A_real"]),
        both(a["L0_cond_A_imag"]), both(a["L0_cond_C"][..., 0]), both(a["L0_cond_C"][..., 1])], axis=1)
    scales = np.stack([a[f"L0_ffn_{n}"].reshape(()) for n in
                       ("gate_in_scale", "up_in_scale", "down_in_scale", "gate_w_scale", "up_w_scale", "down_w_scale")])

    def by_k(w):
        return w.T.reshape(LB, P, I).transpose(1, 0, 2)

    arrays = {
        "in_xT": xt, "in_x": x, "in_length": a["itok_B_78_3631"], "in_params": params, "in_consts": trig_constants(),
        "in_D": a["L0_cond_D"].reshape(1, C), "in_scales": scales,
        "in_gate": by_k(a["L0_ffn_gate_w"]), "in_up": by_k(a["L0_ffn_up_w"]), "in_down": a["L0_ffn_down_w"].T,
    }
    nc = bacc.Bacc("TRN2", target_bir_lowering=False, num_devices=1)
    arrays = {k: np.ascontiguousarray(z) for k, z in arrays.items()}
    args = [nc.dram_tensor(k, z.shape, mybir.dt.from_np(z.dtype), kind="ExternalInput").ap() for k, z in arrays.items()]
    args.append(nc.dram_tensor("out", (B, C, L), F32, kind="ExternalOutput").ap())
    adaln_ffn_kernel(nc, *args)
    r = run_bass_kernel_spmd(nc, [arrays], core_ids=[0])
    return r.results[0]["out"]
```

```python
from contextlib import ExitStack
import math

import numpy as np

import concourse.bass as bass
from concourse import mybir

F32 = mybir.dt.float32
F32R = mybir.dt.float32r
BF16 = mybir.dt.bfloat16
I32 = mybir.dt.int32
ALU = mybir.AluOpType
ACT = mybir.ActivationFunctionType

P = 128
B, C, L = 128, 32, 512
N = 64
I = 1376
HB = 4
NBLK = C // HB
TOK = HB * B
LB = L // P
CH = -(-I // P)
TAIL = I - (CH - 1) * P
PAIRS = (CH + 1) // 2
KA, KB = 16, 32
M = KB + KA
PADK = P - 1
ROW = 640
FP8_MAX = 448.0
K_GROUPS = [range(0, 4), range(4, 16), range(16, 32)]
WARM = 14
READ = 1
EMPTY = 2
UP20 = 2.0 ** 20
FLOOR = 1.5 * 2.0 ** 14
MAGIC = 1.5 * 2.0 ** 23
LOG2E = 1.4426950408889634
LN2_HI = 0.693145751953125
LN2_LO = 0.6931471805599453 - LN2_HI
INV_2PI = 1.0 / (2 * math.pi)
PI2_1 = 6.28125
PI2_2 = 2 * math.pi - PI2_1
PI_IN = 3.1415925


def width(c):
    return P if c < CH - 1 else TAIL


def pair_rows(e):
    return (P, 2) if e < PAIRS - 1 else (TAIL, 1)


def adaln_ffn_kernel(nc, xT, xn, length, params, consts, dskip, scales, wg_d, wu_d, wd_d, out):
    kpad = nc.dram_tensor("kpad_scratch", (2, C, ROW), F32, kind="Internal")
    toep_d = [bass.AP(kpad, i * C * ROW, [[HB * ROW, NBLK], [1, P], [ROW, HB], [1, L]]) for i in range(2)]

    with ExitStack() as ctx:
        def sb(name, shape, dt=F32):
            return ctx.enter_context(nc.sbuf_tensor(name, shape, dt))

        def sem(name):
            return ctx.enter_context(nc.semaphore(name))

        def bank(name):
            return ctx.enter_context(nc.psum_tensor(name, [P, 512], F32))

        gate_ps = [bank(f"gate_ps{i}") for i in range(2)]
        up_ps = [bank(f"up_ps{i}") for i in range(2)]
        down_ps = [bank(f"down_ps{i}") for i in range(2)]
        y_ps = [bank(f"y_ps{i}") for i in range(2)]

        wg = sb("wg", [P, LB, I], BF16)
        wu = sb("wu", [P, LB, I], BF16)
        wd = sb("wd", [P, CH, L], BF16)
        prm = sb("prm", [P, 5 * C])
        cst = sb("cst", [P, M + 5 + LB])
        scl = sb("scl", [P, 6])
        dsk = sb("dsk", [1, C])
        leni = sb("leni", [P, B], I32)
        lenf = sb("lenf", [P, B])
        mask = sb("mask", [P, LB, B])
        fac = sb("fac", [P, 10])
        R_GATE, R_UP, S_GATE, S_UP, S_DOWN, R_DOWN, T_UP, R_GATE20, R_UP20 = range(9)

        sm = sb("sm", [P, 40, C])
        zrow = sb("zrow", [C, P])

        toep = [sb(f"toep{i}", [P, 2, HB, L]) for i in range(2)]
        xhi = [sb(f"xhi{i}", [P, L], F32R) for i in range(2)]
        xlo = [sb(f"xlo{i}", [P, L], F32R) for i in range(2)]
        xt = [sb(f"xt{i}", [P, HB, L]) for i in range(2)]
        xres = [sb(f"xres{i}", [P, HB, L]) for i in range(2)]
        ym = [sb(f"ym{i}", [P, L]) for i in range(2)]
        yv = [sb(f"yv{i}", [P, 2, L]) for i in range(2)]
        yc = [sb(f"yc{i}", [P, 2, L]) for i in range(2)]
        yt = sb("yt", [P, 2, L])
        yq = [sb(f"yq{i}", [P, 2, LB, TOK], BF16) for i in range(2)]
        sil = [sb(f"sil{i}", [P, TOK]) for i in range(2)]
        hv = [sb(f"hv{i}", [P, 2, TOK]) for i in range(2)]
        hc = [sb(f"hc{i}", [P, 2, TOK]) for i in range(2)]
        ht = sb("ht", [P, 2, TOK])
        hq = [sb(f"hq{i}", [P, CH, TOK], BF16) for i in range(2)]

        def inside(tile, lo, n):
            flat = tile[:].rearrange("p a b -> p (a b)")
            flat = flat if flat.dtype == F32 else flat.bitcast(F32)
            return flat[:, C * lo:C * (lo + n)].rearrange("p (c m) -> p c m", m=n)

        ang, g1 = inside(xres[0], 0, M), inside(xres[0], M, KA)
        turns, g2 = inside(xres[1], 0, M), inside(xres[1], M, KA)
        dec, e2 = inside(hq[0], 0, M), inside(hq[0], M, KB)
        esin, gcos, gsin = inside(hq[1], 0, KB), inside(hq[1], KB, KA), inside(hq[1], KB + KA, KA)
        krow = [inside(hc[i], 0, KB)[0:KA] for i in range(2)]

        params_in, consts_in, scales_in = sem("params_in"), sem("consts_in"), sem("scales_in")
        weights_in = sem("weights_in")
        xt_in = [sem(f"xt_in{i}") for i in range(2)]
        conv_in = [sem(f"conv_in{i}") for i in range(2)]
        xres_in = [sem(f"xres_in{i}") for i in range(2)]
        chain = sem("chain")
        zeros_set, k_stored = sem("zeros_set"), [sem(f"k_stored{i}") for i in range(len(K_GROUPS))]
        toep_first = [sem(f"toep_first{h}") for h in range(HB)]
        parts_ready, decay_ready, gabs_ready = sem("parts_ready"), sem("decay_ready"), sem("gabs_ready")
        small_ang_ready, small_sin_ready = sem("small_ang_ready"), sem("small_sin_ready")
        ang_ready, sin_ready = sem("ang_ready"), sem("sin_ready")
        dec_arg_ready, dec_ready, norm_ready = sem("dec_arg_ready"), sem("dec_ready"), sem("norm_ready")
        pool_chain = sem("pool_chain")
        e2_ready, g_ready, scales_ready = sem("e2_ready"), sem("g_ready"), sem("scales_ready")
        k_ready, skip_added, khi_ready, klo_ready = (
            sem("k_ready"), sem("skip_added"), sem("khi_ready"), sem("klo_ready"))
        gate_ready, up_ready, silu_done = sem("gate_ready"), sem("up_ready"), sem("silu_done")
        prod_done, clip_done, abs_ready = sem("prod_done"), sem("clip_done"), sem("abs_ready")
        t_done, hq_ready = sem("t_done"), sem("hq_ready")
        y_ready, ym_done, yscaled = sem("y_ready"), sem("ym_done"), sem("yscaled")
        ymagic_done, yt_done, yq_ready = sem("ymagic_done"), sem("yt_done"), sem("yq_ready")
        yq_first = sem("yq_first")
        xhi_ready, xlo_ready, xlo_dve = sem("xhi_ready"), sem("xlo_ready"), sem("xlo_dve")
        down_ready, out_done = sem("down_ready"), sem("out_done")
        stored = [sem(f"stored{i}") for i in range(2)]

        def at_least(eng, s, v):
            if not (isinstance(v, int) and v <= 0):
                eng.wait_ge(s, v)

        def k_in_bank(i):
            hs = K_GROUPS[i]
            bank = (down_ps[0], down_ps[1], y_ps[1])[i]
            return (bank[0:KA, 0:len(hs) * KB].rearrange("p (h b) -> p h b", b=KB), slice(hs[0], hs[-1] + 1))

        block = ctx.enter_context(nc.Block())

        @block.sync
        def _(sp):
            sp.dma_start(prm[:], params).then_inc(params_in, 16)
            sp.dma_start(cst[:], consts).then_inc(consts_in, 16)
            sp.dma_start(scl[:], scales.partition_broadcast(P)).then_inc(scales_in, 16)
            sp.dma_start(leni[:], length.partition_broadcast(P)).then_inc(scales_in, 16)
            sp.dma_start(dsk[:], dskip).then_inc(scales_in, 16)
            sp.wait_ge(zeros_set, 1)
            for i in range(2):
                sp.dma_start(bass.AP(kpad, i * C * ROW, [[ROW, C], [1, PADK]]), zrow[:, 0:PADK]).then_inc(stored[i], 16)

            def load_x_t(g, par):
                sp.dma_start(xt[par][:], xT[g]).then_inc(xt_in[par], 16)

            def load_toep(g, par):
                for i in range(2):
                    sp.dma_start(toep[par][:, i], toep_d[i][g]).then_inc(conv_in[par], 16)

            def load_res(g, par):
                sp.dma_start(xres[par][:], xn[:, bass.ts(g, HB), :]).then_inc(xres_in[par], 16)

            def store(g, par):
                sp.dma_start(out[:, bass.ts(g, HB), :], xres[par][:]).then_inc(stored[par], 16)

            load_x_t(0, 0)
            load_x_t(1, 1)
            sp.wait_ge(stored[0], 16)
            sp.wait_ge(stored[1], 16)

            def store_k(b):
                lo, n = K_GROUPS[b][0], len(K_GROUPS[b])
                for i in range(2):
                    sp.wait_ge((khi_ready, klo_ready)[i], b + 1)
                    sp.dma_start(bass.AP(kpad, (i * C + lo) * ROW + PADK, [[KB, KA], [ROW, n], [1, KB]]),
                                 krow[i][:, lo:lo + n, :]).then_inc(k_stored[b], 16)

            store_k(0)
            sp.wait_ge(k_stored[0], 32)
            for h in range(HB):
                for i in range(2):
                    sp.dma_start(toep[0][:, i, h], toep_d[i][0, :, h]).then_inc(toep_first[h], 16)
            store_k(1)
            store_k(2)
            load_res(0, 0)
            sp.wait_ge(k_stored[1], 32)
            load_toep(1, 1)
            load_res(1, 1)

            def next_conv(g, par):
                at_least(sp, y_ready, HB * (g - 1))
                load_x_t(g, par)
                load_toep(g, par)

            def turn(g, par, half, conv):
                at_least(sp, out_done, EMPTY + HB * (g - 1))
                store(g - 2, par)
                if conv:
                    next_conv(g + 2, par)
                at_least(sp, stored[par], 16 * (half + 1))
                load_res(g, par)

            next_conv(2, 0)
            next_conv(3, 1)
            with sp.Fori(0, (NBLK - 4) // 2) as j:
                turn(2 * j + 2, 0, j + 1, True)
                turn(2 * j + 3, 1, j + 1, True)
            turn(NBLK - 2, 0, NBLK // 2 - 1, False)
            turn(NBLK - 1, 1, NBLK // 2 - 1, False)
            sp.wait_ge(out_done, EMPTY + HB * (NBLK - 1))
            store(NBLK - 2, 0)
            for t in range(HB):
                sp.wait_ge(out_done, EMPTY + HB * (NBLK - 1) + t + 1)
                sp.dma_start(out[:, HB * (NBLK - 1) + t, :], xres[1][:, t, :]).then_inc(stored[1], 16)
            sp.wait_ge(stored[0], 16 * (NBLK // 2 + 1))
            sp.wait_ge(stored[1], 16 * (NBLK // 2 + HB))

        @block.gpsimd
        def _(pool):
            nc.gpsimd.memset(zrow[:], 0.0).then_inc(zeros_set, 1)
            pool.dma_start(wg[:], wg_d).then_inc(weights_in, 16)
            pool.dma_start(wu[:], wu_d).then_inc(weights_in, 16)
            pool.dma_start(wd[:, 0:CH - 1, :],
                           wd_d[0:(CH - 1) * P, :].rearrange("(k p) n -> p k n", p=P)).then_inc(weights_in, 16)
            pool.dma_start(wd[0:TAIL, CH - 1, :], wd_d[(CH - 1) * P:I, :]).then_inc(weights_in, 16)

            count = [0]

            def link(ins):
                count[0] += 1
                ins.then_inc(pool_chain, 1)
                pool.wait_ge(pool_chain, count[0])

            gp = nc.gpsimd
            pool.wait_ge(decay_ready, 1)
            def s(i):
                return sm[:, i, :]

            link(gp.tensor_scalar(s(19), s(14), -87.0, None, ALU.max))
            link(gp.tensor_scalar(s(20), s(19), LOG2E, MAGIC, ALU.mult, ALU.add))
            link(gp.tensor_scalar(s(20), s(20), MAGIC, None, ALU.subtract))
            for ln2 in (LN2_HI, LN2_LO):
                link(gp.tensor_scalar(s(21), s(20), ln2, None, ALU.mult))
                link(gp.tensor_tensor(s(19), s(19), s(21), ALU.subtract))
            link(gp.tensor_scalar(s(22), s(19), 1.0 / math.factorial(7), None, ALU.mult))
            for d in range(6, 0, -1):
                link(gp.tensor_scalar(s(22), s(22), 1.0 / math.factorial(d), None, ALU.add))
                link(gp.tensor_tensor(s(22), s(22), s(19), ALU.mult))
            link(gp.tensor_scalar(s(23).bitcast(I32), s(20), 127.0, 2.0 ** 23, ALU.add, ALU.mult))
            link(gp.tensor_tensor(s(22), s(22), s(23), ALU.mult))
            link(gp.tensor_scalar(s(23), s(23), -1.0, None, ALU.add))
            link(gp.tensor_tensor(s(24), s(22), s(23), ALU.add))
            gp.tensor_scalar(s(25), s(24), 1.0, None, ALU.add)
            cr, ci, ai = (prm[:, i * C:(i + 1) * C] for i in (3, 4, 2))
            gp.tensor_tensor(s(34), ci, ai, ALU.mult)
            gp.tensor_tensor(s(35), cr, s(9), ALU.mult)
            gp.tensor_tensor(s(36), cr, ai, ALU.mult)
            link(gp.tensor_tensor(s(37), ci, s(9), ALU.mult))
            gp.tensor_tensor(s(34), s(34), s(35), ALU.subtract)
            link(gp.tensor_tensor(s(36), s(36), s(37), ALU.add))
            pool.wait_ge(norm_ready, 1)
            gp.tensor_tensor(s(34), s(34), s(32), ALU.mult)
            gp.tensor_tensor(s(36), s(36), s(32), ALU.mult).then_inc(parts_ready, 1)
            pool.wait_ge(dec_ready, 1)
            pool.wait_ge(sin_ready, 3)
            for i in range(2):
                hs = slice(i * C // 2, (i + 1) * C // 2)
                gp.tensor_tensor(e2[:, hs], esin[:, hs], dec[:, hs, 0:KB], ALU.mult).then_inc(e2_ready, 1)

            def low_part(g, par, h):
                m = HB * g + h
                at_least(pool, xhi_ready, m + 1)
                nc.gpsimd.tensor_tensor(xlo[h % 2][:], xt[par][:, h, :], xhi[h % 2][:].bitcast(F32),
                                        ALU.subtract).then_inc(xlo_ready, 1)

            def round_y(g, par, h, versions=2):
                m = HB * g + h
                q = h % 2
                n = versions
                at_least(pool, ymagic_done, m + 1)
                at_least(pool, yq_ready, m)
                nc.gpsimd.tensor_tensor(yt[:, 0:n], yv[q][:, 0:n], yc[q][:, 0:n], ALU.add).then_inc(yt_done, 1)
                at_least(pool, yt_done, m + 1)
                at_least(pool, up_ready, CH * (g - 1))
                nc.gpsimd.tensor_tensor(
                    yq[par][:, 0:n, :, h * B:(h + 1) * B],
                    yt[:, 0:n].rearrange("p v (k b) -> p v k b", k=LB),
                    yc[q][:, 0:n].rearrange("p v (k b) -> p v k b", k=LB), ALU.subtract).then_inc(yq_ready, 1)

            def turn(g, par, ahead):
                low_part(g, par, 3)
                round_y(g, par, 0)
                round_y(g, par, 1)
                if ahead:
                    low_part(g + 1, 1 - par, 0)
                round_y(g, par, 2)
                round_y(g, par, 3)
                if ahead:
                    low_part(g + 1, 1 - par, 2)

            low_part(0, 0, 0)
            low_part(0, 0, 1)
            low_part(0, 0, 2)
            low_part(0, 0, 3)
            for h in range(HB):
                round_y(0, 0, h, 1)
            low_part(1, 1, 2)
            turn(1, 1, True)
            with pool.Fori(0, (NBLK - 4) // 2) as j:
                turn(2 * j + 2, 0, True)
                turn(2 * j + 3, 1, True)
            turn(NBLK - 2, 0, True)
            turn(NBLK - 1, 1, False)

        @block.scalar
        def _(act):
            act.wait_ge(dec_arg_ready, 1)
            nc.scalar.activation(dec, dec, ACT.Exp).then_inc(dec_ready, 1)
            act.wait_ge(small_ang_ready, 1)
            nc.scalar.activation(sm[:, 12:14, :], sm[:, 10:12, :], ACT.Sin).then_inc(small_sin_ready, 1)
            act.wait_ge(ang_ready, 2)
            nc.scalar.activation(gcos, ang[:, :, KB:], ACT.Abs).then_inc(gabs_ready, 1)
            nc.scalar.activation(gsin, ang[:, :, KB:], ACT.Sin).then_inc(sin_ready, 1)
            act.wait_ge(gabs_ready, 1)
            nc.scalar.activation(gcos, gcos, ACT.Sin, bias=cst[:, M + 4:M + 5], scale=-1.0).then_inc(sin_ready, 1)
            nc.scalar.activation(esin, ang[:, :, 0:KB], ACT.Sin, bias=cst[:, M:M + 1]).then_inc(sin_ready, 1)

            def high_part(g, par, half, h):
                m = HB * g + h
                if h == 0:
                    at_least(act, xt_in[par], 16 * (half + 1))
                at_least(act, y_ready, m - 1)
                nc.scalar.copy(xhi[h % 2][:], xt[par][:, h, :]).then_inc(xhi_ready, 1)

            high_part(0, 0, 0, 0)
            high_part(0, 0, 0, 1)
            for i in range(len(K_GROUPS)):
                act.wait_ge(skip_added, i + 1)
                k_all, hs = k_in_bank(i)
                nc.scalar.copy(krow[0][:, hs, :].bitcast(F32R), k_all).then_inc(khi_ready, 1)

            def scale_y(g, h):
                m = HB * g + h
                q = h % 2
                at_least(act, ym_done, m + 1)
                at_least(act, yt_done, m - 1)
                if isinstance(m, int) and 2 <= m < 2 + HB:
                    act.wait_ge(yq_first, m - 1)
                nc.scalar.activation(yv[q][:, 0, :], ym[q][:], ACT.Copy, scale=fac[:, R_GATE:R_GATE + 1])
                nc.scalar.activation(yv[q][:, 1, :], ym[q][:], ACT.Copy, scale=fac[:, R_UP:R_UP + 1])

            def magnitude_y(g, h):
                m = HB * g + h
                q = h % 2
                at_least(act, yq_ready, m - 1)
                nc.scalar.activation(yc[q][:, 0, :], ym[q][:], ACT.Abs, scale=fac[:, R_GATE20:R_GATE20 + 1])
                nc.scalar.activation(yc[q][:, 1, :], ym[q][:], ACT.Abs,
                                     scale=fac[:, R_UP20:R_UP20 + 1]).then_inc(yscaled, 1)

            def abs_prod(m, e):
                w, n = pair_rows(e)
                at_least(act, clip_done, m + 1)
                at_least(act, hq_ready, m - 1)
                nc.scalar.activation(hc[e % 2][0:w, 0:n], hv[e % 2][0:w, 0:n], ACT.Abs, scale=UP20).then_inc(abs_ready, 1)

            def slots(g, par, half, first, ahead):
                for c in range(CH):
                    n = CH * g + c
                    b = (par + c) % 2
                    w = width(c)
                    at_least(act, gate_ready, n + 1)
                    at_least(act, prod_done, n - 1)
                    nc.scalar.activation(sil[b][0:w, :], gate_ps[b][0:w, :], ACT.Silu,
                                         scale=fac[0:w, S_GATE:S_GATE + 1]).then_inc(silu_done, 1)
                    if c and c % 2 == 0:
                        abs_prod(PAIRS * g + c // 2 - 1, c // 2 - 1)
                    elif c == 0 and not first:
                        abs_prod(PAIRS * g - 1, PAIRS - 1)
                    if c in SPLIT_PLAN and SPLIT_PLAN[c][0] <= ahead:
                        step, h = SPLIT_PLAN[c]
                        high_part(g + step, (par + step) % 2, half + (1 if step == 2 else par), h)
                    if ahead and c in MAGNITUDE_PLAN:
                        magnitude_y(g + 1, MAGNITUDE_PLAN[c][1])
                    if ahead and c in SCALE_PLAN:
                        scale_y(g + 1, SCALE_PLAN[c][1])

            act.wait_ge(scales_ready, 1)
            high_part(0, 0, 0, 2)
            scale_y(0, 0)
            magnitude_y(0, 0)
            high_part(0, 0, 0, 3)
            for stored_k in k_stored:
                act.wait_ge(stored_k, 32)
            scale_y(0, 1)
            magnitude_y(0, 1)
            high_part(1, 1, 0, 0)
            scale_y(0, 2)
            magnitude_y(0, 2)
            high_part(1, 1, 0, 1)
            scale_y(0, 3)
            magnitude_y(0, 3)
            high_part(1, 1, 0, 2)
            slots(0, 0, 0, True, 2)
            with act.Fori(0, (NBLK - 4) // 2) as j:
                slots(2 * j + 1, 1, j, False, 2)
                slots(2 * j + 2, 0, j + 1, False, 2)
            slots(NBLK - 3, 1, (NBLK - 3) // 2, False, 2)
            slots(NBLK - 2, 0, (NBLK - 2) // 2, False, 1)
            slots(NBLK - 1, 1, None, False, 0)
            abs_prod(PAIRS * NBLK - 1, PAIRS - 1)

        @block.tensor
        def _(pe):
            pe.wait_ge(e2_ready, 1)
            pe.wait_ge(g_ready, 1)
            for i, hs in enumerate(K_GROUPS):
                if hs[-1] >= C // 2:
                    pe.wait_ge(e2_ready, 2)
                for h in hs:
                    last = nc.tensor.matmul(k_in_bank(i)[0][:, h - hs[0]], g1[:, h], e2[:, h], start=True, stop=True)
                last.then_inc(k_ready, 1)
            pe.wait_ge(weights_in, 64)
            for n in range(WARM):
                last = nc.tensor.matmul(up_ps[n % 2][:], wg[:, 0, 0:P], wg[:, 0, 0:512], start=True, stop=True)
            last.then_inc(down_ready, READ)

            def conv(g, par, half, h, distances):
                m = HB * g + h
                if distances[0] == 0:
                    if isinstance(m, int) and m < HB:
                        pe.wait_ge(toep_first[h], 32)
                    elif h == 0:
                        at_least(pe, conv_in[par], 32 * (half + par))
                    at_least(pe, ym_done, m - 1)
                    if isinstance(g, int) and g == 0:
                        pe.wait_ge(xlo_ready, h + 1)
                    elif h == 1 or (isinstance(g, int) and g == 1 and h == 0):
                        at_least(pe, xlo_dve, g + h)
                    else:
                        at_least(pe, xlo_ready, 3 * g + (1, 0, 2, 3)[h])
                for d in distances:
                    for part, x in ((0, xhi), (0, xlo), (1, xhi)):
                        last = nc.tensor.matmul(y_ps[h % 2][:, d * P:L],
                                                toep[par][:, part, h, d * P:(d + 1) * P].bitcast(F32R),
                                                x[h % 2][:, 0:L - d * P], start=(d == 0 and part == 0 and x is xhi),
                                                stop=(d == 2 and part == 1))
                if d == 2:
                    last.then_inc(y_ready, 1)

            def down_part(g, par, c):
                for s in range(HB * c, HB * (c + 1)):
                    t, k = divmod(s, CH)
                    w = width(k)
                    if t == 0:
                        at_least(pe, hq_ready, PAIRS * g + k // 2 + 1)
                    if k == 0:
                        at_least(pe, out_done, EMPTY + HB * g + t - 1)
                    mm = nc.tensor.matmul(down_ps[t % 2][:], hq[par][0:w, k, t * P:(t + 1) * P],
                                          wd[0:w, k, :], start=(k == 0), stop=(k == CH - 1))
                    if k == CH - 1:
                        mm.then_inc(down_ready, 1)

            def by_channel(h):
                pe.wait_ge(yq_ready, h + 1)
                pe.wait_ge(yq_first, h + 1)
                cols = slice(h * B, (h + 1) * B)
                for c in range(2):
                    for ps, wt, version, ready in ((gate_ps, wg, 0, gate_ready), (up_ps, wu, 1, up_ready)):
                        for k in range(LB):
                            mm = nc.tensor.matmul(ps[c][:, cols], wt[:, k, c * P:(c + 1) * P],
                                                  yq[0][:, version, k, cols], start=(k == 0), stop=(k == LB - 1))
                        if h == HB - 1:
                            mm.then_inc(ready, 1)

            def slots(g, par, half, down, ahead):
                for c in range(CH):
                    n = CH * g + c
                    b = (par + c) % 2
                    w = width(c)
                    if not (isinstance(n, int) and n < 2):
                        at_least(pe, silu_done, n - 1)
                        at_least(pe, prod_done, n - 1)
                        for lo, hi in (((0, HB - 1), (HB - 1, HB)) if c == 0 else ((0, HB),)):
                            if c == 0:
                                at_least(pe, yq_ready, HB * g + hi)
                            cols = slice(lo * B, hi * B)
                            for ps, wt, version, ready in ((gate_ps, wg, 0, gate_ready), (up_ps, wu, 1, up_ready)):
                                for k in range(LB):
                                    mm = nc.tensor.matmul(ps[b][0:w, cols], wt[:, k, c * P:c * P + w],
                                                          yq[par][:, version, k, cols], start=(k == 0), stop=(k == LB - 1))
                                if hi == HB:
                                    mm.then_inc(ready, 1)
                    for step, h, distances in CONV_PLAN.get(c, ()):
                        if step <= ahead:
                            conv(g + step, (par + step) % 2, half + (1 if step == 2 else par), h, distances)
                    if down:
                        down_part(g - 1, 1 - par, c)

            conv(0, 0, 0, 0, [0, 1, 3, 2])
            pe.wait_ge(khi_ready, len(K_GROUPS))
            pe.wait_ge(klo_ready, len(K_GROUPS))
            for h in range(1, HB):
                conv(0, 0, 0, h, [0, 1, 3, 2])
            by_channel(0)
            by_channel(1)
            conv(1, 1, 0, 0, [0, 1, 3, 2])
            by_channel(2)
            by_channel(3)
            conv(1, 1, 0, 1, [0, 1, 3])
            slots(0, 0, 0, False, 2)
            with pe.Fori(0, (NBLK - 4) // 2) as j:
                slots(2 * j + 1, 1, j, True, 2)
                slots(2 * j + 2, 0, j + 1, True, 2)
            slots(NBLK - 3, 1, (NBLK - 3) // 2, True, 2)
            slots(NBLK - 2, 0, (NBLK - 2) // 2, True, 1)
            slots(NBLK - 1, 1, None, True, 0)
            last_banks = [y_ps[0], y_ps[1], down_ps[0], down_ps[1]]
            early = CH - 3
            for t, chunks in ((0, range(early)), (1, range(early)), (0, range(early, CH)), (1, range(early, CH)),
                              (2, range(CH)), (3, range(CH))):
                for k in chunks:
                    w = width(k)
                    if t == 0:
                        pe.wait_ge(hq_ready, PAIRS * (NBLK - 1) + k // 2 + 1)
                    if t >= 2 and k == 0:
                        pe.wait_ge(out_done, EMPTY + HB * (NBLK - 1) + t - 3)
                    mm = nc.tensor.matmul(last_banks[t][:], hq[1][0:w, k, t * P:(t + 1) * P],
                                          wd[0:w, k, :], start=(k == 0), stop=(k == CH - 1))
                    if k == CH - 1:
                        mm.then_inc(down_ready, 1)

        @block.vector
        def _(dve):
            v = nc.vector
            done = [0]

            def link(ins):
                done[0] += 1
                ins.then_inc(chain, 1)
                dve.wait_ge(chain, done[0])

            def s(i, n=1):
                return sm[:, i:i + n, :]

            def exp_parts(x, kf, r, q, two_k):
                link(v.tensor_scalar(x, x, -87.0, 88.0, ALU.max, ALU.min))
                link(v.tensor_scalar(kf, x, LOG2E, MAGIC, ALU.mult, ALU.add))
                link(v.tensor_scalar(kf, kf, MAGIC, None, ALU.subtract))
                link(v.scalar_tensor_tensor(r, kf, -LN2_HI, x, ALU.mult, ALU.add))
                link(v.scalar_tensor_tensor(r, kf, -LN2_LO, r, ALU.mult, ALU.add))
                link(v.tensor_scalar(q, r, 1.0 / math.factorial(7), None, ALU.mult))
                for d in range(6, 0, -1):
                    link(v.scalar_tensor_tensor(q, q, 1.0 / math.factorial(d), r, ALU.add, ALU.mult))
                link(v.tensor_scalar(two_k.bitcast(I32), kf, 127.0, 2.0 ** 23, ALU.add, ALU.mult))

            v.memset(fac[:], 0.0).then_inc(out_done, EMPTY)
            dve.wait_ge(params_in, 16)
            pr = prm[:].rearrange("p (f h) -> p f h", f=5)
            exp_parts(pr[:, 0:2, :], s(0, 2), s(2, 2), s(4, 2), s(6, 2))
            link(v.scalar_tensor_tensor(s(8, 2), s(4, 2), 1.0, s(6, 2), ALU.add, ALU.mult))
            v.scalar_tensor_tensor(s(14), s(9), -1.0, s(8), ALU.mult, ALU.mult).then_inc(decay_ready, 1)
            link(v.tensor_tensor(s(15), pr[:, 2:3, :], s(8), ALU.mult))
            dve.wait_ge(consts_in, 16)

            def by_h(ap, m):
                return ap.rearrange("p o h -> p h o").broadcast_to([P, C, m])

            multipliers = cst[:, 0:M].rearrange("p (o m) -> p o m", o=1).broadcast_to([P, C, M])
            v.tensor_tensor(dec, by_h(s(14), M), multipliers, ALU.mult).then_inc(dec_arg_ready, 1)
            v.tensor_tensor(ang, by_h(s(15), M), multipliers, ALU.mult)
            ai = pr[:, 2:3, :]
            v.scalar_tensor_tensor(s(32), s(9), 0.5, s(9), ALU.mult, ALU.mult)
            v.scalar_tensor_tensor(s(33), ai, 0.5, ai, ALU.mult, ALU.mult)
            link(v.tensor_scalar(s(16), s(15), 0.5, None, ALU.mult))
            ang_b, ang_a, turns_b, turns_a = ang[:, :, 0:KB], ang[:, :, KB:], turns[:, :, 0:KB], turns[:, :, KB:]
            v.tensor_scalar(turns_b, ang_b, INV_2PI, cst[:, M + 1:M + 2], ALU.mult, ALU.add)
            v.tensor_scalar(turns_a, ang_a, INV_2PI, MAGIC, ALU.mult, ALU.add)
            v.tensor_tensor(s(32), s(32), s(33), ALU.add)
            link(v.tensor_scalar(s(17, 2), s(15, 2), INV_2PI, MAGIC, ALU.mult, ALU.add))
            v.reciprocal(s(32), s(32)).then_inc(norm_ready, 1)
            v.tensor_scalar(turns_b, turns_b, MAGIC, MAGIC, ALU.add, ALU.subtract)
            v.tensor_scalar(turns_a, turns_a, MAGIC, None, ALU.subtract)
            link(v.tensor_scalar(s(17, 2), s(17, 2), MAGIC, None, ALU.subtract))
            v.scalar_tensor_tensor(ang, turns, -PI2_1, ang, ALU.mult, ALU.add)
            link(v.scalar_tensor_tensor(s(10, 2), s(17, 2), -PI2_1, s(15, 2), ALU.mult, ALU.add))
            v.scalar_tensor_tensor(ang, turns, -PI2_2, ang, ALU.mult, ALU.add)
            link(v.scalar_tensor_tensor(s(10, 2), s(17, 2), -PI2_2, s(10, 2), ALU.mult, ALU.add))
            v.tensor_scalar(s(10, 2), s(10, 2), PI_IN, -PI_IN, ALU.min, ALU.max).then_inc(small_ang_ready, 1)
            v.tensor_scalar(ang_a, ang_a, PI_IN, -PI_IN, ALU.min, ALU.max).then_inc(ang_ready, 1)
            v.tensor_scalar(ang_b, ang_b, cst[:, M + 2:M + 3], cst[:, M + 3:M + 4], ALU.min, ALU.max).then_inc(ang_ready, 1)

            dve.wait_ge(parts_ready, 1)
            dve.wait_ge(small_sin_ready, 1)
            link(v.scalar_tensor_tensor(s(26), s(13), -2.0, s(13), ALU.mult, ALU.mult))
            v.tensor_tensor(s(27), s(12), s(25), ALU.mult)
            link(v.tensor_tensor(s(26), s(26), s(25), ALU.mult))
            link(v.tensor_tensor(s(26), s(26), s(24), ALU.add))
            v.tensor_tensor(s(29), s(36), s(27), ALU.mult)
            v.tensor_tensor(s(31), s(34), s(27), ALU.mult)
            v.tensor_tensor(s(28), s(34), s(26), ALU.mult)
            link(v.tensor_tensor(s(30), s(36), s(26), ALU.mult))
            v.tensor_tensor(sm[0:N, 38, :], sm[0:N, 28, :], sm[0:N, 29, :], ALU.add)
            v.tensor_tensor(sm[0:N, 39, :], sm[0:N, 30, :], sm[0:N, 31, :], ALU.subtract)
            v.tensor_tensor(sm[N:P, 38, :], sm[N:P, 30, :], sm[N:P, 31, :], ALU.subtract)
            link(v.scalar_tensor_tensor(sm[N:P, 39, :], sm[N:P, 28, :], -1.0, sm[N:P, 29, :], ALU.mult, ALU.subtract))
            dve.wait_ge(dec_ready, 1)
            dve.wait_ge(sin_ready, 2)
            v.tensor_tensor(g1, gcos, by_h(s(38), KA), ALU.mult)
            link(v.tensor_tensor(g2, gsin, by_h(s(39), KA), ALU.mult))
            link(v.tensor_tensor(g1, g1, g2, ALU.add))
            v.tensor_tensor(g1, g1, dec[:, :, KB:], ALU.mult).then_inc(g_ready, 1)

            dve.wait_ge(scales_in, 48)
            for i in range(len(K_GROUPS)):
                dve.wait_ge(k_ready, i + 1)
                k_all, hs = k_in_bank(i)
                k0 = k_all[0:1, :, 0]
                v.tensor_tensor(k0, k0, dsk[:, hs], ALU.add).then_inc(skip_added, 1)
                dve.wait_ge(khi_ready, i + 1)
                v.tensor_tensor(krow[1][:, hs, :].bitcast(F32R), k_all, krow[0][:, hs, :],
                                ALU.subtract).then_inc(klo_ready, 1)

            def f(i):
                return fac[:, i:i + 1]

            def sc(i):
                return scl[:, i:i + 1]

            v.reciprocal(f(R_GATE), sc(0))
            v.reciprocal(f(R_UP), sc(1))
            v.reciprocal(f(R_DOWN), sc(2))
            v.tensor_tensor(f(S_GATE), sc(0), sc(3), ALU.mult)
            v.tensor_tensor(f(T_UP), sc(1), sc(4), ALU.mult)
            link(v.tensor_tensor(f(S_DOWN), sc(2), sc(5), ALU.mult))
            v.tensor_tensor(f(S_UP), f(T_UP), f(R_DOWN), ALU.mult)
            v.tensor_scalar(f(R_GATE20), f(R_GATE), UP20, None, ALU.mult)
            link(v.tensor_scalar(f(R_UP20), f(R_UP), UP20, None, ALU.mult))

            link(v.tensor_copy(lenf[:], leni[:]))
            for k in range(LB):
                last = v.tensor_scalar(mask[:, k, :], lenf[:], cst[:, M + 5 + k:M + 6 + k], None, ALU.is_gt)
            last.then_inc(scales_ready, 1)
            dve.wait_ge(scales_ready, 1)

            def mask_y(g, h):
                m = HB * g + h
                q = h % 2
                at_least(dve, y_ready, m + 1)
                at_least(dve, yscaled, m - 1)
                v.tensor_tensor(ym[q][:], y_ps[q][:], mask[:].rearrange("p k b -> p (k b)"),
                                ALU.mult).then_inc(ym_done, 1)

            def magic_y(g, h):
                m = HB * g + h
                q = h % 2
                at_least(dve, yscaled, m + 1)
                v.tensor_scalar(yv[q][:], yv[q][:], FP8_MAX, -FP8_MAX, ALU.min, ALU.max)
                v.tensor_scalar(yc[q][:], yc[q][:], FLOOR, FP8_MAX * UP20, ALU.max, ALU.min).then_inc(ymagic_done, 1)

            def first_up(h):
                q = h % 2
                dve.wait_ge(ymagic_done, h + 1)
                link(v.tensor_tensor(ht[:, 0], yv[q][:, 1], yc[q][:, 1], ALU.add))
                v.tensor_tensor(yq[0][:, 1, :, h * B:(h + 1) * B], ht[:, 0].rearrange("p (k b) -> p k b", k=LB),
                                yc[q][:, 1].rearrange("p (k b) -> p k b", k=LB), ALU.subtract).then_inc(yq_first, 1)

            def product(n, par, c):
                b, w = (par + c) % 2, width(c)
                at_least(dve, silu_done, n + 1)
                at_least(dve, up_ready, n + 1)
                v.scalar_tensor_tensor(hv[c // 2 % 2][0:w, c % 2], up_ps[b][0:w, :], fac[0:w, S_UP:S_UP + 1],
                                       sil[b][0:w, :], ALU.mult, ALU.mult).then_inc(prod_done, 1)

            def clip(n, e):
                w, k = pair_rows(e)
                at_least(dve, prod_done, n + 1)
                v.tensor_scalar(hv[e % 2][0:w, 0:k], hv[e % 2][0:w, 0:k], FP8_MAX, -FP8_MAX,
                                ALU.min, ALU.max).then_inc(clip_done, 1)

            def rounded_sum(m, e):
                w, k = pair_rows(e)
                at_least(dve, abs_ready, m + 1)
                at_least(dve, hq_ready, m)
                v.scalar_tensor_tensor(ht[0:w, 0:k], hc[e % 2][0:w, 0:k], FLOOR, hv[e % 2][0:w, 0:k],
                                       ALU.max, ALU.add).then_inc(t_done, 1)

            def rounded(m, g, par, e):
                w, k = pair_rows(e)
                at_least(dve, t_done, m + 1)
                if e == 0:
                    at_least(dve, down_ready, READ + HB * (g - 1))
                v.scalar_tensor_tensor(hq[par][0:w, 2 * e:2 * e + k, :], hc[e % 2][0:w, 0:k], FLOOR, ht[0:w, 0:k],
                                       ALU.max, ALU.subtract, reverse1=True).then_inc(hq_ready, 1)

            def residual(g, par, half, t, ps=None):
                if t == 0:
                    at_least(dve, xres_in[par], 16 * (half + 1))
                at_least(dve, down_ready, READ + HB * g + t + 1)
                v.scalar_tensor_tensor(xres[par][:, t, :], (ps or down_ps[t % 2])[:], f(S_DOWN), xres[par][:, t, :],
                                       ALU.mult, ALU.add).then_inc(out_done, 1)

            def slots(g, par, prev_half, first, ahead):
                for c in range(CH):
                    n = CH * g + c
                    e, m = c // 2, PAIRS * g + c // 2
                    product(n, par, c)
                    if c == 0 and not first:
                        rounded_sum(m - 1, PAIRS - 1)
                        rounded(m - 1, g - 1, 1 - par, PAIRS - 1)
                    final = not ahead and c == CH - 1
                    if final:
                        clip(n, e)
                    if c and c % 2 == 0:
                        rounded_sum(m - 1, e - 1)
                    if (c % 2 or c == CH - 1) and not final:
                        clip(n, e)
                    if (c % 2 and e) or c == CH - 1:
                        rounded(m - 1, g, par, e - 1)
                    if final:
                        rounded_sum(m, e)
                        rounded(m, g, par, e)
                    if c in MASK_PLAN and MASK_PLAN[c][0] <= ahead:
                        mask_y(g + MASK_PLAN[c][0], MASK_PLAN[c][1])
                    if ahead and c in MAGIC_PLAN:
                        magic_y(g + 1, MAGIC_PLAN[c][1])
                    if c == LOW_SLOT and ahead == 2:
                        low_part(g + 2, par, 1)
                    if not first and c in OUT_SLOTS:
                        residual(g - 1, 1 - par, prev_half, OUT_SLOTS.index(c))

            def low_part(g, par, h):
                at_least(dve, xhi_ready, HB * g + h + 1)
                v.tensor_tensor(xlo[h][:], xt[par][:, h, :], xhi[h][:].bitcast(F32),
                                ALU.subtract).then_inc(xlo_dve, 1)

            mask_y(0, 0)
            mask_y(0, 1)
            magic_y(0, 0)
            first_up(0)
            mask_y(0, 2)
            magic_y(0, 1)
            mask_y(0, 3)
            first_up(1)
            low_part(1, 1, 0)
            magic_y(0, 2)
            first_up(2)
            magic_y(0, 3)
            low_part(1, 1, 1)
            first_up(3)
            mask_y(1, 0)
            slots(0, 0, None, True, 2)
            with dve.Fori(0, (NBLK - 4) // 2) as j:
                slots(2 * j + 1, 1, j, False, 2)
                slots(2 * j + 2, 0, j, False, 2)
            slots(NBLK - 3, 1, NBLK // 2 - 2, False, 2)
            slots(NBLK - 2, 0, NBLK // 2 - 2, False, 1)
            slots(NBLK - 1, 1, NBLK // 2 - 1, False, 0)
            for t in range(HB):
                residual(NBLK - 1, 1, NBLK // 2 - 1, t, (y_ps[0], y_ps[1], down_ps[0], down_ps[1])[t])


CONV_PLAN = {
    7: [(2, 0, [0])], 8: [(2, 0, [1, 3])], 9: [(2, 0, [2]), (2, 1, [0])], 10: [(2, 1, [1, 3])],
    0: [(1, 1, [2])], 1: [(1, 2, [0])], 2: [(1, 2, [1, 3])], 3: [(1, 2, [2]), (1, 3, [0])],
    4: [(1, 3, [1, 3])], 5: [(1, 3, [2])],
}
SPLIT_PLAN = {4: (2, 0), 6: (2, 1), 10: (2, 2), 1: (1, 3)}
MASK_PLAN = {9: (2, 0), 0: (1, 1), 3: (1, 2), 5: (1, 3)}
SCALE_PLAN = {0: (1, 0), 1: (1, 1), 4: (1, 2), 6: (1, 3)}
MAGNITUDE_PLAN = {1: (1, 0), 2: (1, 1), 5: (1, 2), 7: (1, 3)}
MAGIC_PLAN = {1: (1, 0), 2: (1, 1), 5: (1, 2), 7: (1, 3)}
LOW_SLOT = 7
OUT_SLOTS = [3, 6, 8, 10]


def trig_constants():
    t = np.zeros((P, M + 5 + LB), np.float32)
    t[:, 0:KB] = np.arange(KB)
    t[:, KB:M] = KB * np.arange(KA)
    phase = np.where(np.arange(P) < N, math.pi / 2, 0.0)
    t[:, M] = phase
    t[:, M + 1] = phase / (2 * math.pi)
    t[:, M + 2] = PI_IN - phase
    t[:, M + 3] = -PI_IN - phase
    t[:, M + 4] = math.pi / 2
    t[:, M + 5:] = np.arange(P)[:, None] + P * np.arange(LB)[None, :]
    return t


def kernel(**inputs):
    import concourse.bacc as bacc
    from concourse.bass_utils import run_bass_kernel_spmd

    a = {k: np.asarray(v) for k, v in inputs.items()}
    x = a["x"]
    xt = x.transpose(1, 2, 0).reshape(NBLK, HB, LB, P, B)[:, :, :, ::-1, :]
    xt = xt.transpose(0, 3, 1, 2, 4).reshape(NBLK, P, HB, L)

    def both(z):
        return np.concatenate([z.T, z.T], axis=0)

    params = np.concatenate([
        np.broadcast_to(a["L0_cond_log_dt"][None, :], (P, C)), both(a["L0_cond_log_A_real"]),
        both(a["L0_cond_A_imag"]), both(a["L0_cond_C"][..., 0]), both(a["L0_cond_C"][..., 1])], axis=1)
    scales = np.stack([a[f"L0_ffn_{n}"].reshape(()) for n in
                       ("gate_in_scale", "up_in_scale", "down_in_scale", "gate_w_scale", "up_w_scale", "down_w_scale")])

    def by_k(w):
        return w.T.reshape(LB, P, I).transpose(1, 0, 2)

    arrays = {
        "in_xT": xt, "in_x": x, "in_length": a["itok_B_78_3631"], "in_params": params, "in_consts": trig_constants(),
        "in_D": a["L0_cond_D"].reshape(1, C), "in_scales": scales,
        "in_gate": by_k(a["L0_ffn_gate_w"]), "in_up": by_k(a["L0_ffn_up_w"]), "in_down": a["L0_ffn_down_w"].T,
    }
    nc = bacc.Bacc("TRN2", target_bir_lowering=False, num_devices=1)
    arrays = {k: np.ascontiguousarray(z) for k, z in arrays.items()}
    args = [nc.dram_tensor(k, z.shape, mybir.dt.from_np(z.dtype), kind="ExternalInput").ap() for k, z in arrays.items()]
    args.append(nc.dram_tensor("out", (B, C, L), F32, kind="ExternalOutput").ap())
    adaln_ffn_kernel(nc, *args)
    r = run_bass_kernel_spmd(nc, [arrays], core_ids=[0])
    return r.results[0]["out"]
```
